# Optimizing a Trainium2 kernel written in Bass

```python
import numpy as np
import jax
import jax.numpy as jnp

def _softmax(x, axis=-1):
    return jax.nn.softmax(x, axis=axis)

def _gelu(x):
    return jax.nn.gelu(x, approximate=True)

def _silu(x):
    return jax.nn.silu(x)

def _sigmoid(x):
    return jax.nn.sigmoid(x)

def _layernorm(x, axis=-1, eps=1e-05):
    m = jnp.mean(x, axis=axis, keepdims=True)
    v = jnp.var(x, axis=axis, keepdims=True)
    return (x - m) / jnp.sqrt(v + eps)

def _scatter_add(tgt, idx, src, axis=0):
    return tgt.at[idx].add(src)

def _segment_sum(src, seg, n):
    return jax.ops.segment_sum(src, seg, n)
kernel_name = 'mk_flamingo_gated_d1_seqx_r8_a2ba96'

def setup_inputs(seed: int=0):
    np.random.seed(seed)
    _w = jnp.asarray

    def _rec_inputs():
        import jax
        import jax.numpy as jnp
        _rk = jax.random.key(seed)
        x = 7.22e-05 + 1 * jax.random.normal(jax.random.fold_in(_rk, 1), (4, 256, 256), jnp.float32)
        _lenS = 256 - jax.random.randint(jax.random.fold_in(_rk, 7), (4,), 0, max(1, 256 // 4) + 1, jnp.int32)
        _lenS2 = 256 - jax.random.randint(jax.random.fold_in(_rk, 8), (4,), 0, max(1, 256 // 4) + 1, jnp.int32)
        _ctx_1024P = jax.random.normal(jax.random.fold_in(_rk, 11), (4, 16, 128), jnp.float32)
        _ctx_1024c = jax.random.dirichlet(jax.random.fold_in(_rk, 511), 0.3 * jnp.ones((16,), jnp.float32), (4, 256))
        _ctx_1024t = jnp.einsum('bsk,bkd->bsd', _ctx_1024c, _ctx_1024P)
        _ctx_1024t = _ctx_1024t * jax.lax.rsqrt(jnp.mean(jnp.square(_ctx_1024t)) + 1e-12) * 0.953939
        ctx_1024 = -1.39393e-06 + 0.999914 * (_ctx_1024t + 0.3 * jax.random.normal(jax.random.fold_in(_rk, 611), (4, 256, 128), jnp.float32))
        fside_BxSx2_0 = jax.random.uniform(jax.random.fold_in(_rk, 12), (4, 256, 2), jnp.float32, 0.0, 0.999707)
        _g = jax.random.normal(jax.random.fold_in(_rk, 9001), (2, 1), jnp.float32)
        _g = jnp.sign(_g) * jnp.maximum(jnp.abs(_g), 1.0) + (_g == 0) * 1.0
        g_xattn = _g[0]
        g_ffn = _g[1]
        return (x, ctx_1024, fside_BxSx2_0, g_xattn, g_ffn)
    x, ctx_1024, fside_BxSx2_0, g_xattn, g_ffn = _rec_inputs()

    def _L0_xattn_setup():
        import jax, jax.numpy as jnp
        import numpy as np
        DIM = 256
        CTX_DIM = 128
        N_HEADS = 32
        HEAD_DIM = DIM // N_HEADS
        POS_DIM = 2
        B, N, CTXN = (2, 256, 256)
        ROPE_BASE = 10000.0

        def apply_axial_rope(x, pos):
            b, n, h, d = x.shape
            p = pos.shape[-1]
            dpa = d // p
            half = dpa // 2
            freqs = ROPE_BASE ** (-jnp.arange(half, dtype=x.dtype) / half)
            ang = pos[..., :, None] * freqs
            cos = jnp.cos(ang)[:, :, None, :, :]
            sin = jnp.sin(ang)[:, :, None, :, :]
            xr = x.reshape(b, n, h, p, half, 2)
            x1, x2 = (xr[..., 0], xr[..., 1])
            out = jnp.stack([x1 * cos - x2 * sin, x1 * sin + x2 * cos], axis=-1)
            return out.reshape(b, n, h, d)
        key = jax.random.key(seed)
        ks = jax.random.split(key, 8)
        x = jax.random.normal(ks[0], (B, N, DIM), jnp.float32)
        ctx = jax.random.normal(ks[1], (B, CTXN, CTX_DIM), jnp.float32)
        pos_map = jax.random.uniform(ks[2], (B, N, POS_DIM), jnp.float32)
        ctx_pos_map = jax.random.uniform(ks[3], (B, CTXN, POS_DIM), jnp.float32)
        Wq = jax.random.normal(ks[4], (DIM, DIM), jnp.float32) / np.sqrt(DIM)
        Wkv = jax.random.normal(ks[5], (CTX_DIM, 2 * DIM), jnp.float32) / np.sqrt(CTX_DIM)
        Wout = jax.random.normal(ks[6], (DIM, DIM), jnp.float32) / np.sqrt(DIM)
        bout = jnp.zeros((DIM,), jnp.float32)
        return {'x': x, 'ctx': ctx, 'pos_map': pos_map, 'ctx_pos_map': ctx_pos_map, 'Wq': Wq, 'Wkv': Wkv, 'Wout': Wout, 'bout': bout}
    _L0_xattn_all = _L0_xattn_setup()
    _L0_xattn_in = {k: v for k, v in _L0_xattn_all.items() if k in ('Wq', 'Wkv', 'Wout', 'bout')}
    del _L0_xattn_all

    def _L0_ffn_setup():
        import jax, jax.numpy as jnp
        import numpy as np
        D_MODEL = 256
        D_HIDDEN = 176
        NUM_SHARED = 2
        NUM_ROUTED = 32
        TOP_K = 6

        def _expert_apply(xf, w1, b1, w2, b2):
            return jnp.maximum(xf @ w1 + b1, 0.0) @ w2 + b2
        key = jax.random.key(seed)
        ks = jax.random.split(key, 11)
        d, h = (D_MODEL, D_HIDDEN)
        s1 = 1.0 / np.sqrt(d)
        s2 = 1.0 / np.sqrt(h)
        x = jax.random.normal(ks[0], (2, 256, d), dtype=jnp.float32)
        sw1 = jax.random.uniform(ks[1], (NUM_SHARED, d, h), jnp.float32, -s1, s1)
        sb1 = jax.random.uniform(ks[2], (NUM_SHARED, h), jnp.float32, -s1, s1)
        sw2 = jax.random.uniform(ks[3], (NUM_SHARED, h, d), jnp.float32, -s2, s2)
        sb2 = jax.random.uniform(ks[4], (NUM_SHARED, d), jnp.float32, -s2, s2)
        rw1 = jax.random.uniform(ks[5], (NUM_ROUTED, d, h), jnp.float32, -s1, s1)
        rb1 = jax.random.uniform(ks[6], (NUM_ROUTED, h), jnp.float32, -s1, s1)
        rw2 = jax.random.uniform(ks[7], (NUM_ROUTED, h, d), jnp.float32, -s2, s2)
        rb2 = jax.random.uniform(ks[8], (NUM_ROUTED, d), jnp.float32, -s2, s2)
        router_w = jax.random.uniform(ks[9], (d, NUM_ROUTED), jnp.float32, -s1, s1)
        router_b = jax.random.uniform(ks[10], (NUM_ROUTED,), jnp.float32, -s1, s1)
        return {'x': x, 'sw1': sw1, 'sb1': sb1, 'sw2': sw2, 'sb2': sb2, 'rw1': rw1, 'rb1': rb1, 'rw2': rw2, 'rb2': rb2, 'router_w': router_w, 'router_b': router_b}
    _L0_ffn_all = _L0_ffn_setup()
    _L0_ffn_in = {k: v for k, v in _L0_ffn_all.items() if k in ('sw1', 'sb1', 'sw2', 'sb2', 'rw1', 'rb1', 'rw2', 'rb2', 'router_w', 'router_b')}
    del _L0_ffn_all
    return {'x': x, 'ctx_1024': ctx_1024, 'fside_BxSx2_0': fside_BxSx2_0, 'g_xattn': g_xattn, 'g_ffn': g_ffn, 'L0_xattn_Wq': _L0_xattn_in['Wq'], 'L0_xattn_Wkv': _L0_xattn_in['Wkv'], 'L0_xattn_Wout': _L0_xattn_in['Wout'], 'L0_xattn_bout': _L0_xattn_in['bout'], 'L0_ffn_sw1': _L0_ffn_in['sw1'], 'L0_ffn_sb1': _L0_ffn_in['sb1'], 'L0_ffn_sw2': _L0_ffn_in['sw2'], 'L0_ffn_sb2': _L0_ffn_in['sb2'], 'L0_ffn_rw1': _L0_ffn_in['rw1'], 'L0_ffn_rb1': _L0_ffn_in['rb1'], 'L0_ffn_rw2': _L0_ffn_in['rw2'], 'L0_ffn_rb2': _L0_ffn_in['rb2'], 'L0_ffn_router_w': _L0_ffn_in['router_w'], 'L0_ffn_router_b': _L0_ffn_in['router_b']}

def reference(x, ctx_1024, fside_BxSx2_0, g_xattn, g_ffn, L0_xattn_Wq, L0_xattn_Wkv, L0_xattn_Wout, L0_xattn_bout, L0_ffn_sw1, L0_ffn_sb1, L0_ffn_sw2, L0_ffn_sb2, L0_ffn_rw1, L0_ffn_rb1, L0_ffn_rw2, L0_ffn_rb2, L0_ffn_router_w, L0_ffn_router_b):
    import jax
    import jax.numpy as jnp

    def _L0_xattn_ref(x, ctx, pos_map, ctx_pos_map, Wq, Wkv, Wout, bout):
        import jax, jax.numpy as jnp
        import numpy as np
        DIM = 256
        CTX_DIM = 128
        N_HEADS = 32
        HEAD_DIM = DIM // N_HEADS
        POS_DIM = 2
        B, N, CTXN = (2, 256, 256)
        ROPE_BASE = 10000.0

        def apply_axial_rope(x, pos):
            b, n, h, d = x.shape
            p = pos.shape[-1]
            dpa = d // p
            half = dpa // 2
            freqs = ROPE_BASE ** (-jnp.arange(half, dtype=x.dtype) / half)
            ang = pos[..., :, None] * freqs
            cos = jnp.cos(ang)[:, :, None, :, :]
            sin = jnp.sin(ang)[:, :, None, :, :]
            xr = x.reshape(b, n, h, p, half, 2)
            x1, x2 = (xr[..., 0], xr[..., 1])
            out = jnp.stack([x1 * cos - x2 * sin, x1 * sin + x2 * cos], axis=-1)
            return out.reshape(b, n, h, d)
        b, n, _ = x.shape
        ctx_n = ctx.shape[1]
        q = (x @ Wq).reshape(b, n, N_HEADS, HEAD_DIM)
        k, v = jnp.split(ctx @ Wkv, 2, axis=-1)
        k = k.reshape(b, ctx_n, N_HEADS, HEAD_DIM)
        v = v.reshape(b, ctx_n, N_HEADS, HEAD_DIM)
        q = apply_axial_rope(q, pos_map)
        k = apply_axial_rope(k, ctx_pos_map)
        scale = 1.0 / np.sqrt(HEAD_DIM).astype(np.float32)
        logits = jnp.einsum('bqhd,bkhd->bhqk', q, k) * scale
        w = jax.nn.softmax(logits, axis=-1)
        attn = jnp.einsum('bhqk,bkhd->bqhd', w, v)
        attn = attn.reshape(b, n, N_HEADS * HEAD_DIM)
        return attn @ Wout + bout

    def _L0_ffn_ref(x, sw1, sb1, sw2, sb2, rw1, rb1, rw2, rb2, router_w, router_b):
        import jax, jax.numpy as jnp
        import numpy as np
        D_MODEL = 256
        D_HIDDEN = 176
        NUM_SHARED = 2
        NUM_ROUTED = 32
        TOP_K = 6

        def _expert_apply(xf, w1, b1, w2, b2):
            return jnp.maximum(xf @ w1 + b1, 0.0) @ w2 + b2
        B, S, d = x.shape
        flat = x.reshape(-1, d)
        T = flat.shape[0]

        def sh_body(acc, p):
            w1, b1, w2, b2 = p
            return (acc + _expert_apply(flat, w1, b1, w2, b2), None)
        shared_out, _ = jax.lax.scan(sh_body, jnp.zeros_like(flat), (sw1, sb1, sw2, sb2))
        shared_out = shared_out / NUM_SHARED
        logits = flat @ router_w + router_b
        probs = jax.nn.softmax(logits, axis=-1)
        topk_p, topk_i = jax.lax.top_k(probs, TOP_K)
        topk_p = topk_p / jnp.sum(topk_p, axis=-1, keepdims=True)
        gates = jnp.zeros((T, NUM_ROUTED), dtype=flat.dtype)
        gates = gates.at[jnp.arange(T)[:, None], topk_i].add(topk_p)

        def r_body(acc, p):
            w1, b1, w2, b2, g = p
            return (acc + g[:, None] * _expert_apply(flat, w1, b1, w2, b2), None)
        routed_out, _ = jax.lax.scan(r_body, jnp.zeros_like(flat), (rw1, rb1, rw2, rb2, gates.T))
        return (shared_out + routed_out).reshape(B, S, d)
    x = x + jnp.tanh(g_xattn[0]) * _L0_xattn_ref(_layernorm(x, axis=-1), ctx_1024, fside_BxSx2_0, fside_BxSx2_0, L0_xattn_Wq, L0_xattn_Wkv, L0_xattn_Wout, L0_xattn_bout)
    x = x + jnp.tanh(g_ffn[0]) * _L0_ffn_ref(_layernorm(x, axis=-1), L0_ffn_sw1, L0_ffn_sb1, L0_ffn_sw2, L0_ffn_sb2, L0_ffn_rw1, L0_ffn_rb1, L0_ffn_rw2, L0_ffn_rb2, L0_ffn_router_w, L0_ffn_router_b)
    return x

_drawn_inputs = setup_inputs


def setup_inputs(seed=0):
    import zlib

    import numpy as np

    out = dict(_drawn_inputs(seed))
    spreads = {'L0_xattn_bout': (0.0, 0.1)}
    factors = {'L0_ffn_sb1': 5.985, 'L0_ffn_rb1': 8.0, 'L0_ffn_rb2': 3.618, 'L0_ffn_router_b': 3.309}
    for name, (base, spread) in spreads.items():
        noise = np.random.default_rng([zlib.crc32(name.encode()), seed]).standard_normal(out[name].shape)
        drawn = base * np.exp(spread * noise) if base else spread * noise
        out[name] = jnp.asarray(drawn.astype(out[name].dtype))
    for name, factor in factors.items():
        out[name] = (out[name] * factor).astype(out[name].dtype)
    return out
```

```python
from contextlib import ExitStack

import numpy as np

import concourse.bass as bass
from concourse import mybir

ALU = mybir.AluOpType
ACT = mybir.ActivationFunctionType
AX = mybir.AxisListType
F32 = mybir.dt.float32
F32R = mybir.dt.float32r
BF16 = mybir.dt.bfloat16

P = 128
BANK = 512


def gated_cross_attention_moe(
    nc, x, ctx, pos, g_xattn, g_ffn, wq, wkv, wout, bout,
    sw1, sb1, sw2, sb2, rw1, rb1, rw2, rb2, router_w, router_b, out,
):
    B, N, D = x.shape
    C = ctx.shape[2]
    HD = 8
    H = D // HD
    NT = B * N // P
    TB = N // P
    KD = D // P
    GH = 4
    HR = P // GH
    NG = H // GH
    GROUPS = B * NG
    TOK = B * N
    HALF = TOK // 2
    SCALE = float(1.0 / np.sqrt(np.float32(HD)))
    EPS = 1e-5
    NS, _, HID = sw1.shape
    NE = rw1.shape[0]
    TOPK = 6
    RT = NE * HID // P
    assert RT * P == NE * HID and HALF == BANK and C == P
    SFULL, SREST = divmod(NS * HID, P)
    SHT = SFULL + 1
    TILES = SHT + RT
    SB_ROW = RT

    R_MAX = 3 * HD

    with ExitStack() as keep:
        def sb(name, shape, dt=F32, where=keep):
            return where.enter_context(nc.sbuf_tensor(name, shape, dt))

        def sem(name):
            return keep.enter_context(nc.semaphore(name))

        x_sb = sb("x_sb", [P, NT, D])
        gx = sb("gx", [P, 1])
        gf = sb("gf", [P, 1])
        ident = sb("ident", [P, P])
        ident_b = sb("ident_b", [P, P], BF16)
        stats = sb("stats", [P, NT, 6])
        mv = sb("mv", [P, NT, 2])
        veps = sb("veps", [P, NT])
        root = sb("root", [P, NT])
        rstd = sb("rstd", [P, NT])
        newton = sb("newton", [P, NT])
        wout_sb = sb("wout_sb", [P, KD, D])
        bout_sb = sb("bout_sb", [P, D])
        rtw_sb = sb("rtw_sb", [P, KD, NE])
        rtb_sb = sb("rtb_sb", [P, NE])
        b1rows = sb("b1rows", [TILES, P])
        b1cols = sb("b1cols", [P, TILES])
        b1half = sb("b1half", [P, SHT])
        b2_sb = sb("b2_sb", [NE + NS, D])
        attn = sb("attn", [P, NT, D])
        w1s = sb("w1s", [P, KD, NS * HID])
        w2s = sb("w2s", [P, SHT, D])

        early = ExitStack()
        def sa(name, shape, dt=F32):
            return sb(name, shape, dt, early)
        wq_sb = sa("wq_sb", [P, KD, D])
        wkv_sb = sa("wkv_sb", [P, 2 * D])
        ctx_sb = sa("ctx_sb", [P, NT, C])
        pos_sb = sa("pos_sb", [P, NT, 2])
        ang = sa("ang", [P, 2, NT * 4])
        turns = sa("turns", [P, 2, NT * 4])
        trig = sa("trig", [P, 2, NT, 4])
        cos8 = sa("cos8", [P, NT, 4, 2])
        sin8 = sa("sin8", [P, NT, 4, 2])
        xn = sa("xn", [P, 2, TB, D])
        xnT = sa("xnT", [P, 2, TB, KD, P])
        ctxT = sa("ctxT", [P, 2, TB, P])
        rot1 = sa("rot1", [P, TB, D])
        rot2 = sa("rot2", [P, TB, D])
        qk32 = sa("qk32", [P, 2, TB, D])
        Qx = sa("Qx", [P, NT, H, HR], F32R)
        Kx = sa("Kx", [P, NT, H, HR], F32R)
        Vx = sa("Vx", [P, NT, H, HR])
        QK = [sa(f"QK{i}", [P, 2, N], F32R) for i in range(4)]
        Kd = [sa(f"Kd{i}", [P, GH, N], F32R) for i in range(4)]
        QT = [sa(f"QT{i}", [P, N], F32R) for i in range(2)]
        nmax = [sa(f"nmax{i}", [P, TB, GH]) for i in range(2)]
        probs = [sa(f"probs{i}", [P, TB, GH, N]) for i in range(2)]
        oT = [sa(f"oT{i}", [P, N]) for i in range(2)]
        rden = [sa(f"rden{i}", [P, TB, GH]) for i in range(2)]
        early.close()

        w1 = sb("w1", [P, KD, NE * HID])
        w2 = sb("w2", [P, RT, D])
        middle = ExitStack()
        attnT = sb("attnT", [P, 2, TB, KD, P], F32, middle)
        proj = sb("proj", [P, TB, D], F32, middle)
        xn2 = sb("xn2", [P, 2, TB, D], F32, middle)
        middle.close()
        hr = [sb(f"hr{i}", [P, HALF]) for i in range(2)]
        hg = [sb(f"hg{i}", [P, HALF]) for i in range(2)]
        w2h = [sb(f"w2h{i}", [P, D], F32R) for i in range(2)]
        xT32 = sb("xT32", [P, KD, TOK])
        xTh = sb("xTh", [P, KD, TOK], F32R)
        xTl = sb("xTl", [P, KD, TOK], F32R)
        late_names = dict(lg=[P, NT, NE], pr=[P, NT, NE], gt=[P, NT, NE], eq=[P, NT, NE], sel=[P, NT, NE])
        lg, pr, gt, eq, sel = (sb(n, s) for n, s in late_names.items())
        PAD = NE // 2
        cum = [sb(f"cum{i}", [P, NT, PAD + NE]) for i in range(2)]
        top8 = sb("top8", [P, NT, 8])
        red = sb("red", [P, 4, NT])
        gates = sb("gates", [P, NT, NE + NS])
        gparts = sb("gparts", [P, NT, 3, NE], BF16)
        gTf = sb("gTf", [NE + NS, TOK])
        gT3 = sb("gT3", [3 * NE, TOK], BF16)
        hot = sb("hot", [3 * NE, NE], BF16)
        owner = sb("owner", [3 * NE, RT * P], BF16)
        w1h = [sb(f"w1h{i}", [P, KD, P], F32R) for i in range(2)]
        w1l = [sb(f"w1l{i}", [P, KD, P], F32R) for i in range(2)]
        w2l = [sb(f"w2l{i}", [P, D], F32R) for i in range(2)]
        hh = [sb(f"hh{i}", [P, TOK], F32R) for i in range(2)]
        hl = [sb(f"hl{i}", [P, TOK], F32R) for i in range(2)]
        yT = xT32
        res = attn

        psum = keep.enter_context(nc.psum_tensor("psum", [P, 8, BANK], F32))
        banks = [psum[:, i, :] for i in range(8)]

        x_ld = [sem(f"x_ld{b}") for b in range(B)]
        pos_ld, ctx_ld, wq_ld, wkv_ld, gate_ld, out_w_ld, bias_ld, b2_ld = (
            sem(n) for n in ("pos_ld", "ctx_ld", "wq_ld", "wkv_ld", "gate_ld", "out_w_ld", "bias_ld", "b2_ld"))
        w1_ld, w2_ld, ws_ld = sem("w1_ld"), sem("w2_ld"), sem("ws_ld")
        b1_clear, ident_ok, pads_ok, pool_step = sem("b1_clear"), sem("ident_ok"), sem("pads_ok"), sem("pool_step")
        dve_step, act_step = sem("dve_step"), sem("act_step")
        veps_ok, root_ok = sem("veps_ok"), sem("root_ok")
        ang_ok, trig_ok, xn_ok, xT_mm, xT_ok, cT_mm, cT_ok = (
            sem(n) for n in ("ang_ok", "trig_ok", "xn_ok", "xT_mm", "xT_ok", "cT_mm", "cT_ok"))
        q_mm, kv_mm, rot_ok, qkv_read, hi_ok, lo_ok, v_ok = (
            sem(n) for n in ("q_mm", "kv_mm", "rot_ok", "qkv_read", "hi_ok", "lo_ok", "v_ok"))
        t_mm, t_ok, s_mm, s_max, mhi_ok, m_ok, t2_mm, q2_ok, st_mm, exp_ok, pv_mm, o_ok, ot_mm, rd_ok, norm_ok = (
            sem(n) for n in ("t_mm", "t_ok", "s_mm", "s_max", "mhi_ok", "m_ok", "t2_mm", "q2_ok",
                             "st_mm", "exp_ok", "pv_mm", "o_ok", "ot_mm", "rd_ok", "norm_ok"))
        kd_ld = [sem(f"kd_ld{i}") for i in range(4)]
        aT_mm, aT_ok, pj_mm, xn2_ok, x2T_mm, x2T_ok, rt_mm, lg_ok, xh_ok, xl_ok, pj_ok = (
            sem(n) for n in ("aT_mm", "aT_ok", "pj_mm", "xn2_ok", "x2T_mm", "x2T_ok", "rt_mm", "lg_ok", "xh_ok", "xl_ok", "pj_ok"))
        b1_mm, b1_ok, sub_ok, pexp_ok, gates_ok, gparts_ok, gT_mm, gTf_ok, gT3_ok, owner_ok = (
            sem(n) for n in ("b1_mm", "b1_ok", "sub_ok", "pexp_ok", "gates_ok", "gparts_ok", "gT_mm", "gTf_ok", "gT3_ok", "owner_ok"))
        hot_ok, ws_hi, ws_ok, h_mm, g_mm, relu_ok, hg_ok, hh_ok, hl_ok, y_mm, act_sync, pool_sync = (
            sem(n) for n in ("hot_ok", "ws_hi", "ws_ok", "h_mm", "g_mm", "relu_ok", "hg_ok", "hh_ok", "hl_ok", "y_mm", "act_sync", "pool_sync"))
        yT_ok, yb_mm, yb_read, res_ok, stored = (
            sem(n) for n in ("yT_ok", "yb_mm", "yb_read", "res_ok", "stored"))

        A_XT, A_CT, A_Q, A_KV, A_B1 = banks[0], banks[1], banks[2], banks[3:5], banks[7]
        A_K = psum[:, 3:5, 0:D]
        S_BANK, ST_BANK, O_BANK, T_BANK, T2_BANK = banks[0:2], banks[2:5], banks[5], banks[6], banks[7]
        C_AT, C_PJ, C_XT, C_RT = banks[0:4]
        Y_BANK = banks[0:4]
        H_BANK, G_BANK = banks[4:6], banks[6:8]
        E_BANK = banks[4:8]

        xf = x.rearrange("b (t p) d -> p (b t) d", p=P)
        of = out.rearrange("b (t p) d -> p (b t) d", p=P)

        def rows_to_partitions(v, n):
            return v.partition_broadcast(n)

        block = keep.enter_context(nc.Block())

        @block.sync
        def _(sp):
            for b in range(B):
                sp.dma_start(x_sb[:, TB * b:TB * b + TB, :], xf[:, TB * b:TB * b + TB, :]).then_inc(x_ld[b], 16)
            sp.dma_start(wq_sb[:, :, :], wq.rearrange("(k p) n -> p k n", p=P)).then_inc(wq_ld, 16)
            sp.dma_start(wkv_sb[:, :], wkv).then_inc(wkv_ld, 16)
            sp.dma_start(wout_sb[:, :, :], wout.rearrange("(k p) n -> p k n", p=P)).then_inc(out_w_ld, 16)
            sp.dma_start(rtw_sb[:, :, :], router_w.rearrange("(k p) n -> p k n", p=P)).then_inc(out_w_ld, 16)
            sp.dma_start(bout_sb[:, :], rows_to_partitions(bout, P)).then_inc(out_w_ld, 16)
            sp.dma_start(rtb_sb[:, :], rows_to_partitions(router_b, P)).then_inc(out_w_ld, 16)
            sp.dma_start(b2_sb[0:NE, :], rb2).then_inc(b2_ld, 16)
            sp.dma_start(b2_sb[NE:NE + NS, :], sb2).then_inc(b2_ld, 16)
            sp.wait_ge(b1_clear, 1)
            sp.dma_start(b1rows[0:RT, :], rb1.rearrange("e h -> (e h)").rearrange("(t p) -> t p", p=P)).then_inc(bias_ld, 16)
            sflat = sb1.rearrange("e h -> (e h)")
            sp.dma_start(b1rows[SB_ROW:SB_ROW + SFULL, :],
                         sflat[0:SFULL * P].rearrange("(t p) -> t p", p=P)).then_inc(bias_ld, 16)
            sp.dma_start(b1rows[SB_ROW + SFULL:TILES, 0:SREST],
                         sflat[SFULL * P:NS * HID].rearrange("(t p) -> t p", t=1)).then_inc(bias_ld, 16)

            sp.wait_ge(pads_ok, 2)
            for i in range(GROUPS):
                sp.wait_ge(t_ok, i + 1)
                if i >= 4:
                    sp.wait_ge(st_mm, 4 * (i - 3))
                for j in range(GH):
                    sp.dma_start(Kd[i % 4][HR * j:HR * j + HR, j, :].bitcast(F32),
                                 QK[i % 4][HR * j:HR * j + HR, 1, :].bitcast(F32)).then_inc(kd_ld[i % 4], 16)
            sp.wait_ge(norm_ok, GROUPS)
            w1v = rw1.rearrange("e (k p) h -> p k e h", p=P)
            w1d = w1[:, :, :].rearrange("p k (e h) -> p k e h", h=HID)
            w2v = rw2.rearrange("e h n -> (e h) n").rearrange("(t p) n -> p t n", p=P)
            for c in range(4):
                e0, e1 = c * NE // 4, (c + 1) * NE // 4
                for k in range(KD):
                    sp.dma_start(w1d[:, k, e0:e1, :], w1v[:, k, e0:e1, :]).then_inc(w1_ld, 16)
                t0, t1 = c * RT // 4, (c + 1) * RT // 4
                sp.dma_start(w2[:, t0:t1, :], w2v[:, t0:t1, :]).then_inc(w2_ld, 16)
            for b in range(B):
                sp.wait_ge(res_ok, b + 1)
                sp.dma_start(of[:, TB * b:TB * b + TB, :], res[:, TB * b:TB * b + TB, :]).then_inc(stored, 16)
            sp.wait_ge(stored, 16 * B)

        @block.gpsimd
        def _(pool):
            steps = [0]

            def then(ins):
                steps[0] += 1
                ins.then_inc(pool_step, 1)
                pool.wait_ge(pool_step, steps[0])

            pool.memset(b1rows[:, :], 0.0).then_inc(b1_clear, 1)
            then(pool.memset(ident[:, :], 0.0))
            then(pool.affine_select(out=ident[:, :], in_=ident[:, :], compare_op=ALU.not_equal, fill=1.0,
                                    base=0, pattern=[[-1, P]], channel_multiplier=1))
            pool.tensor_copy(ident_b[:, :], ident[:, :]).then_inc(ident_ok, 1)
            pool.memset(Qx[:, :, :, R_MAX:HR].bitcast(F32), 0.0).then_inc(pads_ok, 1)
            for i in range(4):
                last = pool.memset(Kd[i][:, :, :].bitcast(F32), 0.0)
            last.then_inc(pads_ok, 1)
            pool.memset(Vx[:, :, :, HD + 1:HR], 0.0).then_inc(pads_ok, 1)
            pool.memset(Vx[:, :, :, HD:HD + 1], 1.0).then_inc(pads_ok, 1)
            for b in range(B):
                pool.wait_ge(hi_ok, 2 * (b + 1))
                rows = slice(TB * b, TB * b + TB)
                q32, k32 = (qk32[:, n].rearrange("p t (h d) -> p t h d", d=HD) for n in range(2))
                pool.tensor_tensor(Qx[:, rows, :, HD:2 * HD], q32, Qx[:, rows, :, 0:HD], ALU.subtract).then_inc(lo_ok, 1)
                pool.tensor_tensor(Kx[:, rows, :, 2 * HD:3 * HD], k32, Kx[:, rows, :, 0:HD], ALU.subtract).then_inc(lo_ok, 1)
            pool.wait_ge(norm_ok, GROUPS)
            then(pool.memset(hot[:, :], 0.0))
            for part in range(3):
                then(pool.affine_select(out=hot[:, :], in_=hot[:, :], compare_op=ALU.not_equal, fill=1.0,
                                        base=-NE * part, pattern=[[-1, NE]], channel_multiplier=1))
            pool.memset(gates[:, :, NE:NE + NS], 1.0 / NS).then_inc(hot_ok, 1)

            pool.wait_ge(ws_ld, 16 * (KD + 2))
            pool.wait_ge(x2T_mm, B)
            for t in range(SHT):
                k = t % 2
                rows = P if t < SFULL else SREST
                src1 = w1s[:, :, P * t:P * t + rows]
                src2 = w2s[0:rows, t, :]
                if t >= 2:
                    pool.wait_ge(h_mm, 2 * t - 2)
                pool.tensor_copy(w1h[k][:, :, 0:rows], src1).then_inc(ws_hi, 1)
                pool.wait_ge(ws_hi, 2 * t + 1)
                pool.tensor_tensor(w1l[k][:, :, 0:rows], src1, w1h[k][:, :, 0:rows], ALU.subtract).then_inc(ws_ok, 1)
                if t >= 2:
                    pool.wait_ge(y_mm, t - 1)
                pool.tensor_copy(w2h[k][0:rows, :], src2).then_inc(ws_hi, 1)
                pool.wait_ge(ws_hi, 2 * t + 2)
                pool.tensor_tensor(w2l[k][0:rows, :], src2, w2h[k][0:rows, :], ALU.subtract).then_inc(ws_ok, 1)
            pool.wait_ge(w1_ld, 16 * 4 * KD)
            pool.wait_ge(w2_ld, 16 * 4)
            with pool.Fori(0, RT // 2) as it:
                for j in range(2):
                    t = it * 2 + (SHT + j)
                    k = (SHT + j) % 2
                    r = it * 2 + j
                    src1 = w1[:, :, bass.ds(r * P, P)]
                    src2 = w2[:, bass.ds(r, 1), :].rearrange("p a n -> p (a n)")
                    pool.wait_ge(h_mm, t * 2 - 2)
                    pool.nop().then_inc(pool_sync, 1)
                    pool.tensor_copy(w1h[k][:, :, :], src1).then_inc(ws_hi, 1)
                    pool.wait_ge(ws_hi, t * 2 + 1)
                    pool.nop().then_inc(pool_sync, 1)
                    pool.tensor_tensor(w1l[k][:, :, :], src1, w1h[k][:, :, :], ALU.subtract).then_inc(ws_ok, 1)
                    pool.wait_ge(y_mm, t - 1)
                    pool.nop().then_inc(pool_sync, 1)
                    pool.tensor_copy(w2h[k][:, :], src2).then_inc(ws_hi, 1)
                    pool.wait_ge(ws_hi, t * 2 + 2)
                    pool.nop().then_inc(pool_sync, 1)
                    pool.tensor_tensor(w2l[k][:, :], src2, w2h[k][:, :], ALU.subtract).then_inc(ws_ok, 1)

        @block.scalar
        def _(act):
            act.dma_start(pos_sb[:, :, :], pos.rearrange("b (t p) a -> p (b t) a", p=P)).then_inc(pos_ld, 16)
            act.dma_start(ctx_sb[:, :, :], ctx.rearrange("b (t p) c -> p (b t) c", p=P)).then_inc(ctx_ld, 16)
            act.dma_start(gx[:, :], rows_to_partitions(g_xattn, P)).then_inc(gate_ld, 16)
            act.dma_start(gf[:, :], rows_to_partitions(g_ffn, P)).then_inc(gate_ld, 16)
            act.wait_ge(ang_ok, 1)
            act.activation(trig[:, :, :, :], ang[:, :, :].rearrange("p s (t f) -> p s t f", f=4), ACT.Sin).then_inc(trig_ok, 1)
            act.wait_ge(veps_ok, 1)
            act.activation(root[:, :], veps[:, :], ACT.Sqrt).then_inc(root_ok, 1)
            act.wait_ge(gate_ld, 32)
            act.activation(gx[:, :], gx[:, :], ACT.Tanh).then_inc(act_step, 1)
            act.activation(gf[:, :], gf[:, :], ACT.Tanh).then_inc(act_step, 1)

            def evacuate(b):
                act.wait_ge(cT_mm, b + 1)
                if b >= 2:
                    act.wait_ge(kv_mm, 2 * (b - 1))
                act.activation(ctxT[:, b % 2], A_CT[:, 0:TB * P].rearrange("p (t q) -> p t q", t=TB), ACT.Copy).then_inc(cT_ok, 1)
                act.wait_ge(xT_mm, b + 1)
                if b >= 2:
                    act.wait_ge(q_mm, b - 1)
                act.activation(xnT[:, b % 2], A_XT[:, :].rearrange("p (t k q) -> p t k q", t=TB, k=KD), ACT.Copy).then_inc(xT_ok, 1)

            def high_parts(b):
                rows = slice(TB * b, TB * b + TB)
                act.wait_ge(kv_mm, TB * (b + 1))
                for t in range(TB):
                    act.activation(Vx[:, TB * b + t, :, 0:HD], A_KV[t][:, D:2 * D].rearrange("p (h d) -> p h d", d=HD),
                                   ACT.Copy).then_inc(v_ok, 1)
                q32, k32 = (qk32[:, n].rearrange("p t (h d) -> p t h d", d=HD) for n in range(2))
                act.wait_ge(rot_ok, 2 * b + 1)
                act.activation(Qx[:, rows, :, 0:HD], q32, ACT.Copy).then_inc(hi_ok, 1)
                act.activation(Qx[:, rows, :, 2 * HD:3 * HD], q32, ACT.Copy)
                act.wait_ge(rot_ok, 2 * b + 2)
                act.activation(Kx[:, rows, :, 0:HD], k32, ACT.Copy).then_inc(hi_ok, 1)
                act.activation(Kx[:, rows, :, HD:2 * HD], k32, ACT.Copy).then_inc(qkv_read, 1)

            evacuate(0)
            evacuate(1)
            for k in range(KD):
                act.dma_start(w1s[:, k, :].rearrange("p (e h) -> p e h", h=HID),
                              sw1.rearrange("e (k p) h -> p k e h", p=P)[:, k]).then_inc(ws_ld, 16)
            sflat2 = sw2.rearrange("e h n -> (e h) n")
            act.dma_start(w2s[:, 0:SFULL, :], sflat2[0:SFULL * P, :].rearrange("(t p) n -> p t n", p=P)).then_inc(ws_ld, 16)
            act.dma_start(w2s[0:SREST, SFULL, :], sflat2[SFULL * P:NS * HID, :]).then_inc(ws_ld, 16)
            high_parts(0)
            for b in range(1, B):
                if b + 1 < B:
                    evacuate(b + 1)
                high_parts(b)

            def evacuate_t(i):
                act.wait_ge(t_mm, i + 1)
                if i >= 4:
                    act.wait_ge(s_mm, 4 * (i - 3))
                    act.wait_ge(kd_ld[i % 4], 64 * (i // 4))
                act.activation(QK[i % 4][:, :, :], T_BANK[:, :].rearrange("p (a n) -> p a n", a=2), ACT.Copy).then_inc(t_ok, 1)

            def step(i):
                if i + 2 < GROUPS:
                    evacuate_t(i + 2)
                g = i - 1
                if 0 <= g < GROUPS:
                    act.wait_ge(t2_mm, g + 1)
                    if g >= 2:
                        act.wait_ge(st_mm, 4 * (g - 1))
                    act.activation(QT[g % 2][:, :], T2_BANK[:, 0:N], ACT.Copy).then_inc(q2_ok, 1)
                g = i - 2
                if 0 <= g < GROUPS:
                    act.wait_ge(pv_mm, 2 * (g + 1))
                    if g >= 2:
                        act.wait_ge(ot_mm, g - 1)
                    act.activation(oT[g % 2][:, :], O_BANK[:, 0:N], ACT.Copy).then_inc(o_ok, 1)
                g = i - 1
                if 0 <= g < GROUPS:
                    if g >= 2:
                        act.wait_ge(pv_mm, 2 * (g - 1))
                    for n in range(4):
                        kt, hp = n // 2, n % 2
                        act.wait_ge(st_mm, 4 * g + n + 1)
                        act.activation(probs[g % 2][:, kt, 2 * hp:2 * hp + 2, :],
                                       ST_BANK[(4 * g + n) % 3][:, :].rearrange("p (h q) -> p h q", h=2),
                                       ACT.Exp, scale=SCALE).then_inc(exp_ok, 1)

            evacuate_t(0)
            evacuate_t(1)
            for i in range(GROUPS + 3):
                step(i)

            act.wait_ge(norm_ok, GROUPS)
            for s in range(B + 1):
                if s < B:
                    act.wait_ge(aT_mm, s + 1)
                    if s >= 2:
                        act.wait_ge(pj_mm, s - 1)
                    act.activation(attnT[:, s % 2], C_AT[:, :].rearrange("p (t k q) -> p t k q", t=TB, k=KD),
                                   ACT.Copy).then_inc(aT_ok, 1)
                    act.wait_ge(veps_ok, s + 2)
                    rows = slice(TB * s, TB * s + TB)
                    act.activation(root[:, rows], veps[:, rows], ACT.Sqrt).then_inc(root_ok, 1)
                b = s - 1
                if b >= 0:
                    act.wait_ge(x2T_mm, b + 1)
                    for t in range(TB):
                        cols = slice((TB * b + t) * P, (TB * b + t + 1) * P)
                        act.activation(xT32[:, :, cols],
                                       C_XT[:, KD * P * t:KD * P * (t + 1)].rearrange("p (k q) -> p k q", k=KD),
                                       ACT.Copy).then_inc(x2T_ok, 1)
                    act.wait_ge(x2T_ok, TB * (b + 1))
                    cols = slice(TB * b * P, TB * (b + 1) * P)
                    act.activation(xTh[:, :, cols], xT32[:, :, cols], ACT.Copy).then_inc(xh_ok, 1)
            act.wait_ge(sub_ok, 1)
            act.activation(pr[:, :, :], lg[:, :, :], ACT.Exp).then_inc(pexp_ok, 1)
            act.wait_ge(hot_ok, 1)
            act.activation(owner[:, :].rearrange("p (e h) -> p e h", h=HID),
                           hot[:, :].unsqueeze(2).to_broadcast([3 * NE, NE, HID]), ACT.Copy).then_inc(owner_ok, 1)

            act.wait_ge(b1_ok, 2)

            def relu_static(u):
                t, half = u // 2, u % 2
                rows = P if t < SFULL else SREST
                act.wait_ge(h_mm, u + 1)
                if u >= 2:
                    act.wait_ge(hl_ok, u - 1)
                act.activation(hr[half][0:rows, :], H_BANK[half][0:rows, :], ACT.Relu,
                               bias=b1half[0:rows, t:t + 1], scale=1.0 / NS).then_inc(relu_ok, 1)

            for u in range(2 * SHT):
                relu_static(u)
            for half in range(2):
                act.wait_ge(gT_mm, half + 1)
                act.activation(gTf[:, half * HALF:(half + 1) * HALF], G_BANK[half][0:NE + NS, :],
                               ACT.Copy).then_inc(gTf_ok, 1)
            with act.Fori(0, RT // 2) as it:
                for j in range(2):
                    for half in range(2):
                        u = it * 4 + (2 * (SHT + j) + half)
                        act.wait_ge(h_mm, u + 1)
                        act.wait_ge(hl_ok, u - 1)
                        act.nop().then_inc(act_sync, 1)
                        act.activation(hr[half][:, :], H_BANK[half][:, :], ACT.Relu,
                                       bias=b1cols[:, bass.ds(it * 2 + j, 1)]).then_inc(relu_ok, 1)
            act.wait_ge(y_mm, TILES + 1)
            for k in range(KD):
                act.activation(yT[:, k, 0:HALF], Y_BANK[2 * k][:, :], ACT.Copy).then_inc(yT_ok, 1)

        @block.vector
        def _(dve):
            steps = [0]

            def then(ins):
                steps[0] += 1
                ins.then_inc(dve_step, 1)
                dve.wait_ge(dve_step, steps[0])

            TWO_PI = 2 * np.pi
            C1 = float(np.float32(6.28125))
            C2 = float(np.float32(TWO_PI - 6.28125))
            ROUND = float(1.5 * 2 ** 23)
            PI_BELOW = float(np.nextafter(np.float32(np.pi), np.float32(0)))
            FREQ1 = float(np.float32(10000.0) ** np.float32(-0.5))

            dve.wait_ge(pos_ld, 16)
            sine = ang[:, 0].rearrange("p (t a f) -> p t a f", a=2, f=2)
            dve.tensor_scalar(sine[:, :, :, 0], pos_sb[:, :, :], 1.0, None, ALU.mult)
            then(dve.tensor_scalar(sine[:, :, :, 1], pos_sb[:, :, :], FREQ1, None, ALU.mult))
            then(dve.tensor_scalar(ang[:, 1], ang[:, 0], float(np.pi / 2), None, ALU.add))
            then(dve.tensor_scalar(turns[:, :, :], ang[:, :, :], float(1 / TWO_PI), ROUND, ALU.mult, ALU.add))
            then(dve.tensor_scalar(turns[:, :, :], turns[:, :, :], ROUND, None, ALU.subtract))
            then(dve.scalar_tensor_tensor(out=ang[:, :, :], in0=turns[:, :, :], scalar=-C1, in1=ang[:, :, :],
                                          op0=ALU.mult, op1=ALU.add))
            then(dve.scalar_tensor_tensor(out=ang[:, :, :], in0=turns[:, :, :], scalar=-C2, in1=ang[:, :, :],
                                          op0=ALU.mult, op1=ALU.add))
            dve.tensor_scalar(ang[:, :, :], ang[:, :, :], PI_BELOW, -PI_BELOW, ALU.min, ALU.max).then_inc(ang_ok, 1)

            roots = [0]

            def inverse_deviation(first, n):
                rows = slice(first, first + n)
                for t in range(first, first + n):
                    ins = dve.bn_stats(stats[:, t, :], x_sb[:, t, :])
                then(ins)
                for t in range(first, first + n):
                    ins = dve.bn_aggr(mv[:, t, :], stats[:, t, :])
                then(ins)
                dve.tensor_scalar(veps[:, rows], mv[:, rows, 1], EPS, None, ALU.add).then_inc(veps_ok, 1)
                roots[0] += 1
                dve.wait_ge(root_ok, roots[0])
                then(dve.reciprocal(rstd[:, rows], root[:, rows]))
                then(dve.tensor_tensor(newton[:, rows], rstd[:, rows], rstd[:, rows], ALU.mult))
                then(dve.tensor_tensor(newton[:, rows], newton[:, rows], veps[:, rows], ALU.mult))
                then(dve.tensor_scalar(newton[:, rows], newton[:, rows], -0.5, 1.5, ALU.mult, ALU.add))
                then(dve.tensor_tensor(rstd[:, rows], rstd[:, rows], newton[:, rows], ALU.mult))

            def normalise_rows(b, dst, done):
                for t in range(TB):
                    n = TB * b + t
                    dve.tensor_scalar(dst[:, b % 2, t, :], x_sb[:, n, :], mv[:, n, 0:1], rstd[:, n:n + 1],
                                      ALU.subtract, ALU.mult).then_inc(done, 1)

            def norm_1(b):
                if b >= 2:
                    dve.wait_ge(xT_mm, b - 1)
                normalise_rows(b, xn, xn_ok)

            def rotate(b, n, psum):
                rows = slice(TB * b, TB * b + TB)
                c8, s8 = (v[:, rows].rearrange("p t f c -> p t (f c)").unsqueeze(2).to_broadcast([P, TB, H, 8])
                          for v in (cos8, sin8))
                src = psum.rearrange("p t (h d) -> p t h d", d=HD)
                t1, t2 = (v[:, :, :].rearrange("p t (h d) -> p t h d", d=HD) for v in (rot1, rot2))
                if 2 * b + n:
                    dve.wait_ge(rot_ok, 2 * b + n)
                dve.tensor_tensor(t1, src, c8, ALU.mult)
                then(dve.tensor_tensor(t2, src, s8, ALU.mult))
                pairs = [v.rearrange("p t (m c) -> p (t m) c", c=2) for v in (rot1[:, :, :], rot2[:, :, :], qk32[:, n])]
                if b:
                    dve.wait_ge(qkv_read, b)
                    dve.wait_ge(lo_ok, 2 * b)
                dve.tensor_tensor(pairs[2][:, :, 0], pairs[0][:, :, 0], pairs[1][:, :, 1], ALU.add)
                dve.tensor_tensor(pairs[2][:, :, 1], pairs[0][:, :, 1], pairs[1][:, :, 0], ALU.add).then_inc(rot_ok, 1)

            for b in range(B):
                dve.wait_ge(x_ld[b], 16)
            inverse_deviation(0, NT)
            norm_1(0)
            norm_1(1)
            dve.memset(Kx[:, :, :, R_MAX:R_MAX + 2].bitcast(F32), 1.0)
            dve.memset(Kx[:, :, :, R_MAX + 2:HR].bitcast(F32), 0.0).then_inc(pads_ok, 1)
            dve.wait_ge(trig_ok, 1)
            dve.tensor_copy(cos8[:, :, :, :], trig[:, 1].unsqueeze(3).to_broadcast([P, NT, 4, 2]))
            dve.tensor_copy(sin8[:, :, :, 0], trig[:, 0])
            then(dve.tensor_scalar(sin8[:, :, :, 1], trig[:, 0], -1.0, None, ALU.mult))
            for b in range(B):
                dve.wait_ge(q_mm, b + 1)
                rotate(b, 0, A_Q[:, :].rearrange("p (t n) -> p t n", t=TB))
                dve.wait_ge(v_ok, TB * (b + 1))
                rotate(b, 1, A_K)
                if b + 2 < B:
                    norm_1(b + 2)
            dve.wait_ge(b1_mm, 1)
            dve.tensor_copy(b1cols[:, :], A_B1[:, 0:TILES]).then_inc(b1_ok, 1)
            dve.tensor_scalar(b1half[:, :], A_B1[:, SB_ROW:TILES], 1.0 / NS, None, ALU.mult).then_inc(b1_ok, 1)

            def row_max(i, n):
                qt, hp = n // 2, n % 2
                if n == 0 and i >= 2:
                    dve.wait_ge(m_ok, i - 1)
                dve.wait_ge(s_mm, 4 * i + n + 1)
                dve.tensor_reduce(nmax[i % 2][:, qt, 2 * hp:2 * hp + 2],
                                  S_BANK[n % 2][:, :].rearrange("p (h k) -> p h k", h=2),
                                  AX.X, ALU.max, negate=True).then_inc(s_max, 1)

            def normalise(i):
                b, g = i // NG, i % NG
                o = T2_BANK[:, 0:TB * P].rearrange("p (t h c) -> p t h c", t=TB, h=GH)
                if i >= 2:
                    dve.wait_ge(norm_ok, i - 1)
                dve.wait_ge(ot_mm, i + 1)
                dve.reciprocal(rden[i % 2][:, :, :], o[:, :, :, HD]).then_inc(rd_ok, 1)
                dve.wait_ge(rd_ok, i + 1)
                dst = attn[:, TB * b:TB * b + TB, GH * HD * g:GH * HD * (g + 1)].rearrange("p t (h d) -> p t h d", d=HD)
                dve.tensor_tensor(dst, o[:, :, :, 0:HD],
                                  rden[i % 2][:, :, :].unsqueeze(3).to_broadcast([P, TB, GH, HD]),
                                  ALU.mult).then_inc(norm_ok, 1)

            for i in range(GROUPS + 3):
                if i < GROUPS:
                    row_max(i, 0)
                    row_max(i, 1)
                if 0 <= i - 3:
                    normalise(i - 3)
                if i < GROUPS:
                    row_max(i, 2)
                    row_max(i, 3)
                    b, g = i // NG, i % NG
                    dst = Qx[:, TB * b:TB * b + TB, GH * g:GH * g + GH, :]
                    dve.wait_ge(s_max, 4 * i + 4)
                    dve.tensor_copy(dst[:, :, :, R_MAX], nmax[i % 2][:, :, :]).then_inc(mhi_ok, 1)
                    dve.wait_ge(mhi_ok, i + 1)
                    dve.tensor_tensor(dst[:, :, :, R_MAX + 1], nmax[i % 2][:, :, :], dst[:, :, :, R_MAX],
                                      ALU.subtract).then_inc(m_ok, 1)

            dve.wait_ge(act_step, 2)
            dve.wait_ge(out_w_ld, 64)
            for s in range(B + 2):
                if s < B:
                    rows = slice(TB * s, TB * s + TB)
                    dve.wait_ge(pj_mm, s + 1)
                    dve.tensor_tensor(proj[:, :, :], C_PJ[:, :].rearrange("p (t n) -> p t n", t=TB),
                                      bout_sb[:, :].unsqueeze(1).to_broadcast([P, TB, D]), ALU.add).then_inc(pj_ok, 1)
                    dve.wait_ge(pj_ok, s + 1)
                    then(dve.scalar_tensor_tensor(out=x_sb[:, rows, :], in0=proj[:, :, :], scalar=gx[:, 0:1],
                                                  in1=x_sb[:, rows, :], op0=ALU.mult, op1=ALU.add))
                    if s >= 2:
                        dve.wait_ge(x2T_mm, s - 1)
                    inverse_deviation(TB * s, TB)
                    normalise_rows(s, xn2, xn2_ok)
                b = s - 2
                if b >= 0:
                    cols = slice(TB * b * P, TB * (b + 1) * P)
                    dve.wait_ge(xh_ok, b + 1)
                    dve.tensor_tensor(xTl[:, :, cols], xT32[:, :, cols], xTh[:, :, cols], ALU.subtract).then_inc(xl_ok, 1)
                    dve.wait_ge(rt_mm, b + 1)
                    dve.tensor_tensor(lg[:, TB * b:TB * b + TB, :],
                                      C_RT[:, 0:TB * NE].rearrange("p (t e) -> p t e", t=TB),
                                      rtb_sb[:, :].unsqueeze(1).to_broadcast([P, TB, NE]), ALU.add).then_inc(lg_ok, 1)

            def per_expert(v):
                return v.unsqueeze(2).to_broadcast([P, NT, NE])

            dve.wait_ge(lg_ok, B)
            then(dve.tensor_reduce(red[:, 0], lg[:, :, :], AX.X, ALU.max))
            dve.tensor_tensor(lg[:, :, :], lg[:, :, :], per_expert(red[:, 0]), ALU.subtract).then_inc(sub_ok, 1)
            for c in cum:
                dve.memset(c[:, :, 0:PAD], 0.0)
            dve.wait_ge(pexp_ok, 1)
            then(dve.tensor_reduce(red[:, 1], pr[:, :, :], AX.X, ALU.add))
            then(dve.reciprocal(red[:, 2], red[:, 1]))
            then(dve.tensor_tensor(pr[:, :, :], pr[:, :, :], per_expert(red[:, 2]), ALU.mult))
            for t in range(NT):
                ins = dve.max(top8[:, t, :], pr[:, t, :])
            then(ins)
            sixth = per_expert(top8[:, :, TOPK - 1])
            then(dve.tensor_tensor(gt[:, :, :], pr[:, :, :], sixth, ALU.is_gt))
            dve.tensor_reduce(red[:, 3], gt[:, :, :], AX.X, ALU.add)
            dve.tensor_tensor(eq[:, :, :], pr[:, :, :], sixth, ALU.is_equal)
            then(dve.tensor_tensor(cum[0][:, :, PAD:], pr[:, :, :], sixth, ALU.is_equal))
            then(dve.tensor_scalar(red[:, 0], red[:, 3], -1.0, float(TOPK), ALU.mult, ALU.add))
            shift, a = 1, 0
            while shift < NE:
                then(dve.tensor_tensor(cum[1 - a][:, :, PAD:], cum[a][:, :, PAD:],
                                       cum[a][:, :, PAD - shift:PAD + NE - shift], ALU.add))
                shift, a = 2 * shift, 1 - a
            then(dve.tensor_tensor(sel[:, :, :], cum[a][:, :, PAD:], per_expert(red[:, 0]), ALU.is_le))
            then(dve.tensor_tensor(eq[:, :, :], eq[:, :, :], sel[:, :, :], ALU.mult))
            then(dve.tensor_tensor(gt[:, :, :], gt[:, :, :], eq[:, :, :], ALU.add))
            then(dve.tensor_tensor(sel[:, :, :], gt[:, :, :], pr[:, :, :], ALU.mult))
            then(dve.tensor_reduce(red[:, 1], sel[:, :, :], AX.X, ALU.add))
            then(dve.reciprocal(red[:, 2], red[:, 1]))
            dve.wait_ge(hot_ok, 1)
            then(dve.tensor_tensor(gates[:, :, 0:NE], sel[:, :, :], per_expert(red[:, 2]), ALU.mult))
            then(dve.tensor_copy(gparts[:, :, 0, :], gates[:, :, 0:NE]))
            then(dve.tensor_tensor(sel[:, :, :], gates[:, :, 0:NE], gparts[:, :, 0, :], ALU.subtract))
            then(dve.tensor_copy(gparts[:, :, 1, :], sel[:, :, :]))
            then(dve.tensor_tensor(sel[:, :, :], sel[:, :, :], gparts[:, :, 1, :], ALU.subtract))
            dve.tensor_copy(gparts[:, :, 2, :], sel[:, :, :]).then_inc(gparts_ok, 1)

            for u in range(2 * SHT):
                t, half = u // 2, u % 2
                rows = P if t < SFULL else SREST
                cols = slice(half * HALF, (half + 1) * HALF)
                if t >= 2:
                    dve.wait_ge(y_mm, t - 1)
                dve.wait_ge(relu_ok, u + 1)
                dve.tensor_copy(hh[t % 2][0:rows, cols], hr[half][0:rows, :]).then_inc(hh_ok, 1)
                dve.wait_ge(hh_ok, u + 1)
                dve.tensor_tensor(hl[t % 2][0:rows, cols], hr[half][0:rows, :], hh[t % 2][0:rows, cols],
                                  ALU.subtract).then_inc(hl_ok, 1)
            dve.wait_ge(gT_mm, 3)
            dve.tensor_copy(gT3[:, :], G_BANK[0].bitcast(BF16)[0:3 * NE, :]).then_inc(gT3_ok, 1)
            with dve.Fori(0, RT // 2) as it:
                for j in range(2):
                    for half in range(2):
                        tt = SHT + j
                        u = it * 4 + (2 * tt + half)
                        r = it * 4 + (2 * j + half)
                        cols = slice(half * HALF, (half + 1) * HALF)
                        dve.wait_ge(hl_ok, u - 1)
                        dve.wait_ge(g_mm, r + 1)
                        dve.wait_ge(relu_ok, u + 1)
                        dve.tensor_tensor(hg[half][:, :], hr[half][:, :], G_BANK[half][:, :], ALU.mult).then_inc(hg_ok, 1)
                        dve.wait_ge(y_mm, it * 2 + (tt - 1))
                        dve.wait_ge(hg_ok, r + 1)
                        dve.tensor_copy(hh[tt % 2][:, cols], hg[half][:, :]).then_inc(hh_ok, 1)
                        dve.wait_ge(hh_ok, u + 1)
                        dve.tensor_tensor(hl[tt % 2][:, cols], hg[half][:, :], hh[tt % 2][:, cols],
                                          ALU.subtract).then_inc(hl_ok, 1)
            dve.wait_ge(y_mm, TILES + 1)
            for k in range(KD):
                dve.tensor_copy(yT[:, k, HALF:TOK], Y_BANK[2 * k + 1][:, :]).then_inc(yT_ok, 1)
            for b in range(B):
                rows = slice(TB * b, TB * b + TB)
                dve.wait_ge(yb_mm, b + 1)
                dve.scalar_tensor_tensor(out=res[:, rows, :], in0=E_BANK[b].rearrange("p (t n) -> p t n", t=TB),
                                         scalar=gf[:, 0:1], in1=x_sb[:, rows, :],
                                         op0=ALU.mult, op1=ALU.add).then_inc(res_ok, 1)

        @block.tensor
        def _(pe):
            pe.wait_ge(ident_ok, 1)
            for s in range(B + 1):
                if s < B:
                    if s == 0:
                        pe.wait_ge(ctx_ld, 16)
                    else:
                        pe.wait_ge(cT_ok, s)
                    for t in range(TB):
                        ins = pe.transpose(A_CT[:, t * P:(t + 1) * P], ctx_sb[:, TB * s + t, :], ident[:, :])
                    ins.then_inc(cT_mm, 1)
                    pe.wait_ge(xn_ok, TB * (s + 1))
                    if s:
                        pe.wait_ge(xT_ok, s)
                    for t in range(TB):
                        for k in range(KD):
                            n = (t * KD + k) * P
                            ins = pe.transpose(A_XT[:, n:n + P], xn[:, s % 2, t, k * P:(k + 1) * P], ident[:, :])
                    ins.then_inc(xT_mm, 1)
                b = s - 1
                if b >= 0:
                    pe.wait_ge(cT_ok, b + 1)
                    pe.wait_ge(wkv_ld, 16)
                    if b:
                        pe.wait_ge(rot_ok, 2 * b)
                        pe.wait_ge(v_ok, TB * b)
                    for t in range(TB):
                        pe.matmul(A_KV[t], ctxT[:, b % 2, t, :], wkv_sb[:, :], start=True, stop=True).then_inc(kv_mm, 1)
                    pe.wait_ge(xT_ok, b + 1)
                    pe.wait_ge(wq_ld, 16)
                    for t in range(TB):
                        for k in range(KD):
                            ins = pe.matmul(A_Q[:, t * D:(t + 1) * D], xnT[:, b % 2, t, k, :], wq_sb[:, k, :],
                                            start=(k == 0), stop=(k == KD - 1))
                    ins.then_inc(q_mm, 1)
            pe.wait_ge(bias_ld, 48)
            pe.transpose(A_B1[:, 0:TILES], b1rows[:, :], ident[0:TILES, 0:TILES]).then_inc(b1_mm, 1)

            def transposes(i):
                b, g = i // NG, i % NG
                if g == 0:
                    pe.wait_ge(qkv_read, b + 1)
                    pe.wait_ge(lo_ok, 2 * (b + 1))
                if i:
                    pe.wait_ge(t_ok, i)
                for a, src in enumerate((Qx, Kx)):
                    for t in range(TB):
                        n = (a * TB + t) * P
                        ins = pe.transpose(T_BANK[:, n:n + P],
                                           src[:, TB * b + t, GH * g:GH * g + GH, :].rearrange("p h r -> p (h r)").bitcast(F32),
                                           ident[:, :])
                ins.then_inc(t_mm, 1)

            def scores(i, n):
                qt, hp = n // 2, n % 2
                if n == 0:
                    pe.wait_ge(kd_ld[i % 4], 64 * (i // 4 + 1))
                    pe.wait_ge(t_ok, i + 1)
                if 4 * i + n >= 2:
                    pe.wait_ge(s_max, 4 * i + n - 1)
                pe.matmul(S_BANK[n % 2], QK[i % 4][:, 0, qt * P:(qt + 1) * P], Kd[i % 4][:, 2 * hp:2 * hp + 2, :],
                          start=True, stop=True).then_inc(s_mm, 1)

            def transposes_with_max(i):
                b, g = i // NG, i % NG
                pe.wait_ge(m_ok, i + 1)
                if i >= 2:
                    pe.wait_ge(norm_ok, i - 1)
                for t in range(TB):
                    ins = pe.transpose(T2_BANK[:, t * P:(t + 1) * P],
                                       Qx[:, TB * b + t, GH * g:GH * g + GH, :].rearrange("p h r -> p (h r)").bitcast(F32),
                                       ident[:, :])
                ins.then_inc(t2_mm, 1)

            def shifted_scores(i, n):
                kt, hp = n // 2, n % 2
                if n == 0:
                    pe.wait_ge(q2_ok, i + 1)
                if 4 * i + n >= 3:
                    pe.wait_ge(exp_ok, 4 * i + n - 2)
                for h in range(2):
                    ins = pe.matmul(ST_BANK[(4 * i + n) % 3][:, h * N:(h + 1) * N],
                                    Kd[i % 4][:, 2 * hp + h, kt * P:(kt + 1) * P], QT[i % 2][:, :], start=True, stop=True)
                ins.then_inc(st_mm, 1)

            def values(i, kt):
                b, g = i // NG, i % NG
                pe.wait_ge(exp_ok, 4 * i + 2 * (kt + 1))
                if kt == 0 and i:
                    pe.wait_ge(o_ok, i)
                for h in range(GH):
                    ins = pe.matmul(O_BANK[HR * h:HR * h + HR, 0:N], Vx[:, TB * b + kt, GH * g + h, :],
                                    probs[i % 2][:, kt, h, :], start=(kt == 0), stop=(kt == TB - 1))
                ins.then_inc(pv_mm, 1)

            def outputs(i):
                pe.wait_ge(o_ok, i + 1)
                pe.wait_ge(q2_ok, min(i + 2, GROUPS))
                if i:
                    pe.wait_ge(norm_ok, i)
                for t in range(TB):
                    ins = pe.transpose(T2_BANK[:, t * P:(t + 1) * P], oT[i % 2][:, t * P:(t + 1) * P], ident[:, :])
                ins.then_inc(ot_mm, 1)

            transposes(0)
            transposes(1)
            pe.wait_ge(pads_ok, 5)
            pe.wait_ge(rot_ok, 2 * B)
            pe.wait_ge(v_ok, NT)
            pe.wait_ge(b1_ok, 2)
            for i in range(GROUPS + 3):
                if i < GROUPS:
                    scores(i, 0)
                    scores(i, 1)
                if i >= 3:
                    outputs(i - 3)
                if i + 2 < GROUPS:
                    transposes(i + 2)
                if 0 <= i - 2 < GROUPS:
                    values(i - 2, 0)
                if i < GROUPS:
                    scores(i, 2)
                if 0 <= i - 1 < GROUPS:
                    transposes_with_max(i - 1)
                if 0 <= i - 2 < GROUPS:
                    values(i - 2, 1)
                if i < GROUPS:
                    scores(i, 3)
                if 0 <= i - 1 < GROUPS:
                    for n in range(4):
                        shifted_scores(i - 1, n)

            pe.wait_ge(norm_ok, GROUPS)
            pe.wait_ge(out_w_ld, 64)
            for s in range(B + 2):
                if s < B:
                    if s:
                        pe.wait_ge(aT_ok, s)
                    for t in range(TB):
                        for k in range(KD):
                            n = (t * KD + k) * P
                            ins = pe.transpose(C_AT[:, n:n + P], attn[:, TB * s + t, k * P:(k + 1) * P], ident[:, :])
                    ins.then_inc(aT_mm, 1)
                    pe.wait_ge(aT_ok, s + 1)
                    if s:
                        pe.wait_ge(pj_ok, s)
                    for t in range(TB):
                        for k in range(KD):
                            ins = pe.matmul(C_PJ[:, t * D:(t + 1) * D], attnT[:, s % 2, t, k, :], wout_sb[:, k, :],
                                            start=(k == 0), stop=(k == KD - 1))
                    ins.then_inc(pj_mm, 1)
                b = s - 1
                if 0 <= b < B:
                    pe.wait_ge(xn2_ok, TB * (b + 1))
                    if b:
                        pe.wait_ge(x2T_ok, TB * b)
                    for t in range(TB):
                        for k in range(KD):
                            n = (t * KD + k) * P
                            ins = pe.transpose(C_XT[:, n:n + P], xn2[:, b % 2, t, k * P:(k + 1) * P], ident[:, :])
                    ins.then_inc(x2T_mm, 1)
                b = s - 2
                if b >= 0:
                    pe.wait_ge(x2T_ok, TB * (b + 1))
                    if b:
                        pe.wait_ge(lg_ok, b)
                    for t in range(TB):
                        for k in range(KD):
                            n = (TB * b + t) * P
                            ins = pe.matmul(C_RT[:, t * NE:(t + 1) * NE], xT32[:, k, n:n + P], rtw_sb[:, k, :],
                                            start=(k == 0), stop=(k == KD - 1))
                    ins.then_inc(rt_mm, 1)

            def hidden(t, k2, rows, r=None):
                for half in range(2):
                    u = t * 2 + half
                    if not isinstance(t, int) or t:
                        pe.wait_ge(relu_ok, u - 1)
                        pe.wait_ge(hl_ok, u - 1)
                    pe.wait_ge(ws_ok, t * 2 + 1)
                    cols = slice(half * HALF, (half + 1) * HALF)
                    parts = [(w, v, k) for w, v in ((w1h, xTh), (w1l, xTh), (w1h, xTl)) for k in range(KD)]
                    for n, (w, v, k) in enumerate(parts):
                        ins = pe.matmul(H_BANK[half][0:rows, :], w[k2][:, k, 0:rows], v[:, k, cols],
                                        start=(n == 0), stop=(n == len(parts) - 1))
                    ins.then_inc(h_mm, 1)
                    if r is not None:
                        pe.matmul(G_BANK[half], owner[:, bass.ds(r * P, P)], gT3[:, cols],
                                  start=True, stop=True).then_inc(g_mm, 1)

            def result(t, k2, rows, first=False):
                pe.wait_ge(ws_ok, t * 2 + 2)
                for half in range(2):
                    pe.wait_ge(hl_ok, t * 2 + half + 1)
                    cols = slice(half * HALF, (half + 1) * HALF)
                    for k in range(KD):
                        wc = slice(k * P, (k + 1) * P)
                        for n, (w, v) in enumerate(((w2h, hh), (w2l, hh), (w2h, hl))):
                            ins = pe.matmul(Y_BANK[2 * k + half], w[k2][0:rows, wc], v[k2][0:rows, cols],
                                            start=(first and n == 0), stop=False, skip_group_check=True)
                ins.then_inc(y_mm, 1)

            pe.wait_ge(xh_ok, B)
            pe.wait_ge(xl_ok, B)
            hidden(0, 0, P)
            pe.wait_ge(lg_ok, B)
            for t in range(SHT - 1):
                hidden(t + 1, (t + 1) % 2, P if t + 1 < SFULL else SREST)
                result(t, t % 2, P, first=(t == 0))
            pe.wait_ge(gparts_ok, 1)
            for half in range(2):
                for c in range(NT // 2):
                    t = half * (NT // 2) + c
                    ins = pe.transpose(G_BANK[half][0:NE + NS, c * P:(c + 1) * P], gates[:, t, :], ident[:, :])
                ins.then_inc(gT_mm, 1)
            pe.wait_ge(gTf_ok, 1)
            for t in range(NT):
                ins = pe.transpose(G_BANK[0].bitcast(BF16)[0:3 * NE, t * P:(t + 1) * P],
                                   gparts[:, t].rearrange("p a e -> p (a e)"), ident_b[:, :])
            ins.then_inc(gT_mm, 1)
            pe.wait_ge(gTf_ok, 2)
            pe.wait_ge(gT3_ok, 1)
            pe.wait_ge(owner_ok, 1)
            hidden(SHT, SHT % 2, P, r=0)
            result(SHT - 1, (SHT - 1) % 2, SREST)
            with pe.Fori(0, RT // 2 - 1) as it:
                for j in range(2):
                    t = it * 2 + (SHT + j)
                    hidden(t + 1, (SHT + j + 1) % 2, P, r=it * 2 + (j + 1))
                    result(t, (SHT + j) % 2, P)
            hidden(TILES - 1, (TILES - 1) % 2, P, r=RT - 1)
            result(TILES - 2, (TILES - 2) % 2, P)
            result(TILES - 1, (TILES - 1) % 2, P)
            pe.wait_ge(b2_ld, 32)
            for k in range(KD):
                for half in range(2):
                    ins = pe.matmul(Y_BANK[2 * k + half], b2_sb[:, k * P:(k + 1) * P],
                                    gTf[:, half * HALF:(half + 1) * HALF], start=False, stop=True, skip_group_check=True)
            ins.then_inc(y_mm, 1)
            for b in range(B):
                pe.wait_ge(yT_ok, 4)
                for t in range(TB):
                    for k in range(KD):
                        n = (TB * b + t) * P
                        ins = pe.transpose(E_BANK[b][:, (t * KD + k) * P:(t * KD + k + 1) * P],
                                           yT[:, k, n:n + P], ident[:, :])
                ins.then_inc(yb_mm, 1)


_INS = ['x', 'ctx_1024', 'fside_BxSx2_0', 'g_xattn', 'g_ffn', 'L0_xattn_Wq', 'L0_xattn_Wkv', 'L0_xattn_Wout',
        'L0_xattn_bout', 'L0_ffn_sw1', 'L0_ffn_sb1', 'L0_ffn_sw2', 'L0_ffn_sb2', 'L0_ffn_rw1', 'L0_ffn_rb1',
        'L0_ffn_rw2', 'L0_ffn_rb2', 'L0_ffn_router_w', 'L0_ffn_router_b']
_OUTS = [((4, 256, 256), 'float32')]


def kernel(**inputs):
    import numpy as _np
    import concourse.bacc as _bacc
    from concourse import mybir as _mybir
    from concourse.bass_utils import run_bass_kernel_spmd as _run

    nc = _bacc.Bacc("TRN2", target_bir_lowering=False, num_devices=1)
    arrays, args = {}, []
    for name in _INS:
        a = _np.ascontiguousarray(inputs[name])
        arrays[f"in_{name}_dram"] = a
        args.append(nc.dram_tensor(f"in_{name}_dram", a.shape, _mybir.dt.from_np(a.dtype), kind="ExternalInput").ap())
    for i, (shape, dtype) in enumerate(_OUTS):
        dt = _mybir.dt.from_np(_np.dtype(dtype))
        args.append(nc.dram_tensor(f"out_{i}_dram", shape, dt, kind="ExternalOutput").ap())
    gated_cross_attention_moe(nc, *args)
    r = _run(nc, [arrays], core_ids=[0])
    got = tuple(r.results[0][f"out_{i}_dram"] for i in range(len(_OUTS)))
    return got[0]
```

```python
from contextlib import ExitStack

import numpy as np

import concourse.bass as bass
from concourse import mybir

ALU = mybir.AluOpType
ACT = mybir.ActivationFunctionType
AX = mybir.AxisListType
F32 = mybir.dt.float32
F32R = mybir.dt.float32r
BF16 = mybir.dt.bfloat16

P = 128
BANK = 512


def gated_cross_attention_moe(
    nc, x, ctx, pos, g_xattn, g_ffn, wq, wkv, wout, bout,
    sw1, sb1, sw2, sb2, rw1, rb1, rw2, rb2, router_w, router_b, out,
):
    B, N, D = x.shape
    C = ctx.shape[2]
    HD = 8
    H = D // HD
    NT = B * N // P
    TB = N // P
    KD = D // P
    GH = 4
    HR = P // GH
    NG = H // GH
    GROUPS = B * NG
    TOK = B * N
    HALF = TOK // 2
    SCALE = float(1.0 / np.sqrt(np.float32(HD)))
    EPS = 1e-5
    NS, _, HID = sw1.shape
    NE = rw1.shape[0]
    TOPK = 6
    RT = NE * HID // P
    assert RT * P == NE * HID and HALF == BANK and C == P
    SFULL, SREST = divmod(NS * HID, P)
    SHT = SFULL + 1
    TILES = SHT + RT
    SB_ROW = RT

    R_MAX = 3 * HD

    with ExitStack() as keep:
        def sb(name, shape, dt=F32, where=keep):
            return where.enter_context(nc.sbuf_tensor(name, shape, dt))

        def sem(name):
            return keep.enter_context(nc.semaphore(name))

        x_sb = sb("x_sb", [P, NT, D])
        gx = sb("gx", [P, 1])
        gf = sb("gf", [P, 1])
        ident = sb("ident", [P, P])
        ident_b = sb("ident_b", [P, P], BF16)
        stats = sb("stats", [P, NT, 6])
        mv = sb("mv", [P, NT, 2])
        veps = sb("veps", [P, NT])
        root = sb("root", [P, NT])
        rstd = sb("rstd", [P, NT])
        newton = sb("newton", [P, NT])
        wout_sb = sb("wout_sb", [P, KD, D])
        bout_sb = sb("bout_sb", [P, D])
        rtw_sb = sb("rtw_sb", [P, KD, NE])
        rtb_sb = sb("rtb_sb", [P, NE])
        b1rows = sb("b1rows", [TILES, P])
        b1cols = sb("b1cols", [P, TILES])
        b1half = sb("b1half", [P, SHT])
        b2_sb = sb("b2_sb", [NE + NS, D])
        attn = sb("attn", [P, NT, D])
        w1s = sb("w1s", [P, KD, NS * HID])
        w2s = sb("w2s", [P, SHT, D])

        early = ExitStack()
        def sa(name, shape, dt=F32):
            return sb(name, shape, dt, early)
        wq_sb = sa("wq_sb", [P, KD, D])
        wkv_sb = sa("wkv_sb", [P, 2 * D])
        ctx_sb = sa("ctx_sb", [P, NT, C])
        pos_sb = sa("pos_sb", [P, NT, 2])
        ang = sa("ang", [P, 2, NT * 4])
        turns = sa("turns", [P, 2, NT * 4])
        trig = sa("trig", [P, 2, NT, 4])
        cos8 = sa("cos8", [P, NT, 4, 2])
        sin8 = sa("sin8", [P, NT, 4, 2])
        xn = sa("xn", [P, B, TB, D])
        xnT = sa("xnT", [P, B, TB, KD, P])
        ctxT = sa("ctxT", [P, NT, P])
        rot1 = sa("rot1", [P, TB, D])
        rot2 = sa("rot2", [P, TB, D])
        qk32 = sa("qk32", [P, 2, TB, D])
        Qx = sa("Qx", [P, NT, H, HR], F32R)
        Kx = sa("Kx", [P, NT, H, HR], F32R)
        Vx = sa("Vx", [P, NT, H, HR])
        QK = [sa(f"QK{i}", [P, 2, N], F32R) for i in range(4)]
        Kd = [sa(f"Kd{i}", [P, GH, N], F32R) for i in range(4)]
        QT = [sa(f"QT{i}", [P, N], F32R) for i in range(2)]
        nmax = [sa(f"nmax{i}", [P, TB, GH]) for i in range(2)]
        probs = [sa(f"probs{i}", [P, TB, GH, N]) for i in range(2)]
        oT = [sa(f"oT{i}", [P, N]) for i in range(2)]
        rden = [sa(f"rden{i}", [P, TB, GH]) for i in range(2)]
        early.close()

        w1 = sb("w1", [P, KD, NE * HID])
        w2 = sb("w2", [P, RT, D])
        middle = ExitStack()
        attnT = sb("attnT", [P, 2, TB, KD, P], F32, middle)
        xn2 = sb("xn2", [P, 2, TB, D], F32, middle)
        middle.close()
        hr = [sb(f"hr{i}", [P, HALF]) for i in range(2)]
        hg = [sb(f"hg{i}", [P, HALF]) for i in range(2)]
        xT32 = sb("xT32", [P, KD, TOK])
        xTh = sb("xTh", [P, KD, TOK], F32R)
        xTl = sb("xTl", [P, KD, TOK], F32R)
        late_names = dict(lg=[P, NT, NE], pr=[P, NT, NE], gt=[P, NT, NE], eq=[P, NT, NE], sel=[P, NT, NE])
        lg, pr, gt, eq, sel = (sb(n, s) for n, s in late_names.items())
        PAD = NE // 2
        cum = [sb(f"cum{i}", [P, NT, PAD + NE]) for i in range(2)]
        top8 = sb("top8", [P, NT, 8])
        red = sb("red", [P, 4, NT])
        gates = sb("gates", [P, NT, NE + NS])
        gparts = sb("gparts", [P, NT, 3, NE], BF16)
        gTf = sb("gTf", [NE + NS, TOK])
        gT3 = sb("gT3", [3 * NE, TOK], BF16)
        hot = sb("hot", [3 * NE, NE], BF16)
        owner = sb("owner", [3 * NE, RT * P], BF16)
        w1h = [sb(f"w1h{i}", [P, KD, P], F32R) for i in range(2)]
        w1l = [sb(f"w1l{i}", [P, KD, P], F32R) for i in range(2)]
        w2h = [sb(f"w2h{i}", [P, D], F32R) for i in range(2)]
        w2l = [sb(f"w2l{i}", [P, D], F32R) for i in range(2)]
        hh = [sb(f"hh{i}", [P, TOK], F32R) for i in range(2)]
        hl = [sb(f"hl{i}", [P, TOK], F32R) for i in range(2)]
        yT = xT32
        res = attn

        psum = keep.enter_context(nc.psum_tensor("psum", [P, 8, BANK], F32))
        banks = [psum[:, i, :] for i in range(8)]

        x_ld = [sem(f"x_ld{b}") for b in range(B)]
        pos_ld, ctx_ld, wq_ld, wkv_ld, gate_ld, out_w_ld, bias_ld, b2_ld = (
            sem(n) for n in ("pos_ld", "ctx_ld", "wq_ld", "wkv_ld", "gate_ld", "out_w_ld", "bias_ld", "b2_ld"))
        w1_ld, w2_ld, ws_ld = sem("w1_ld"), sem("w2_ld"), sem("ws_ld")
        b1_clear, ident_ok, pads_ok, pool_step = sem("b1_clear"), sem("ident_ok"), sem("pads_ok"), sem("pool_step")
        dve_step, act_step = sem("dve_step"), sem("act_step")
        veps_ok, root_ok = sem("veps_ok"), sem("root_ok")
        ang_ok, trig_ok, xn_ok, xT_mm, xT_ok, cT_mm, cT_ok = (
            sem(n) for n in ("ang_ok", "trig_ok", "xn_ok", "xT_mm", "xT_ok", "cT_mm", "cT_ok"))
        q_mm, kv_mm, rot_ok, qkv_read, hi_ok, lo_ok, v_ok = (
            sem(n) for n in ("q_mm", "kv_mm", "rot_ok", "qkv_read", "hi_ok", "lo_ok", "v_ok"))
        t_mm, t_ok, s_mm, s_max, mhi_ok, m_ok, t2_mm, q2_ok, st_mm, exp_ok, pv_mm, o_ok, ot_mm, rd_ok, norm_ok = (
            sem(n) for n in ("t_mm", "t_ok", "s_mm", "s_max", "mhi_ok", "m_ok", "t2_mm", "q2_ok",
                             "st_mm", "exp_ok", "pv_mm", "o_ok", "ot_mm", "rd_ok", "norm_ok"))
        kd_ld = [sem(f"kd_ld{i}") for i in range(4)]
        aT_mm, aT_ok, pj_mm, xn2_ok, x2T_mm, x2T_ok, rt_mm, lg_ok, xh_ok, xl_ok, pj_ok, xb_ok = (
            sem(n) for n in ("aT_mm", "aT_ok", "pj_mm", "xn2_ok", "x2T_mm", "x2T_ok", "rt_mm", "lg_ok", "xh_ok", "xl_ok", "pj_ok", "xb_ok"))
        b1_mm, b1_ok, sub_ok, pexp_ok, gates_ok, gparts_ok, gT_mm, gTf_ok, gT3_ok, owner_ok = (
            sem(n) for n in ("b1_mm", "b1_ok", "sub_ok", "pexp_ok", "gates_ok", "gparts_ok", "gT_mm", "gTf_ok", "gT3_ok", "owner_ok"))
        hot_ok, ws_hi, ws_ok, h_mm, g_mm, relu_ok, hg_ok, hh_ok, hl_ok, y_mm, act_sync, pool_sync = (
            sem(n) for n in ("hot_ok", "ws_hi", "ws_ok", "h_mm", "g_mm", "relu_ok", "hg_ok", "hh_ok", "hl_ok", "y_mm", "act_sync", "pool_sync"))
        yT_ok, yb_mm, yb_read, res_ok, stored = (
            sem(n) for n in ("yT_ok", "yb_mm", "yb_read", "res_ok", "stored"))

        A_CT, A_XT, A_Q, A_B1 = banks[0:2], banks[6:8], banks[0:2], banks[7]
        A_KV = [psum[:, 2:4, :], psum[:, 4:6, :]]
        S_BANK, ST_BANK, O_BANK, T_BANK, T2_BANK = banks[0:2], banks[2:5], banks[5], banks[6], banks[7]
        C_AT, C_PJ, C_XT, C_RT = banks[0:2], banks[2:4], banks[4:6], banks[6]
        Y_BANK = banks[0:4]
        H_BANK, G_BANK = banks[4:6], banks[6:8]
        E_BANK = banks[4:8]

        xf = x.rearrange("b (t p) d -> p (b t) d", p=P)
        of = out.rearrange("b (t p) d -> p (b t) d", p=P)

        def rows_to_partitions(v, n):
            return v.partition_broadcast(n)

        block = keep.enter_context(nc.Block())

        @block.sync
        def _(sp):
            for b in range(B):
                sp.dma_start(x_sb[:, TB * b:TB * b + TB, :], xf[:, TB * b:TB * b + TB, :]).then_inc(x_ld[b], 16)
            sp.dma_start(wq_sb[:, :, :], wq.rearrange("(k p) n -> p k n", p=P)).then_inc(wq_ld, 16)
            sp.dma_start(wkv_sb[:, :], wkv).then_inc(wkv_ld, 16)
            sp.dma_start(wout_sb[:, :, :], wout.rearrange("(k p) n -> p k n", p=P)).then_inc(out_w_ld, 16)
            sp.dma_start(rtw_sb[:, :, :], router_w.rearrange("(k p) n -> p k n", p=P)).then_inc(out_w_ld, 16)
            sp.dma_start(bout_sb[:, :], rows_to_partitions(bout, P)).then_inc(out_w_ld, 16)
            sp.dma_start(rtb_sb[:, :], rows_to_partitions(router_b, P)).then_inc(out_w_ld, 16)
            sp.dma_start(b2_sb[0:NE, :], rb2).then_inc(b2_ld, 16)
            sp.dma_start(b2_sb[NE:NE + NS, :], sb2).then_inc(b2_ld, 16)
            sp.wait_ge(b1_clear, 1)
            sp.dma_start(b1rows[0:RT, :], rb1.rearrange("e h -> (e h)").rearrange("(t p) -> t p", p=P)).then_inc(bias_ld, 16)
            sflat = sb1.rearrange("e h -> (e h)")
            sp.dma_start(b1rows[SB_ROW:SB_ROW + SFULL, :],
                         sflat[0:SFULL * P].rearrange("(t p) -> t p", p=P)).then_inc(bias_ld, 16)
            sp.dma_start(b1rows[SB_ROW + SFULL:TILES, 0:SREST],
                         sflat[SFULL * P:NS * HID].rearrange("(t p) -> t p", t=1)).then_inc(bias_ld, 16)

            sp.wait_ge(pads_ok, 2)
            for i in range(GROUPS):
                sp.wait_ge(t_ok, i + 1)
                if i >= 4:
                    sp.wait_ge(st_mm, 4 * (i - 3))
                for j in range(GH):
                    sp.dma_start(Kd[i % 4][HR * j:HR * j + HR, j, :].bitcast(F32),
                                 QK[i % 4][HR * j:HR * j + HR, 1, :].bitcast(F32)).then_inc(kd_ld[i % 4], 16)
            sp.wait_ge(norm_ok, GROUPS)
            w1v = rw1.rearrange("e (k p) h -> p k e h", p=P)
            w1d = w1[:, :, :].rearrange("p k (e h) -> p k e h", h=HID)
            w2v = rw2.rearrange("e h n -> (e h) n").rearrange("(t p) n -> p t n", p=P)
            for c in range(4):
                e0, e1 = c * NE // 4, (c + 1) * NE // 4
                for k in range(KD):
                    sp.dma_start(w1d[:, k, e0:e1, :], w1v[:, k, e0:e1, :]).then_inc(w1_ld, 16)
                t0, t1 = c * RT // 4, (c + 1) * RT // 4
                sp.dma_start(w2[:, t0:t1, :], w2v[:, t0:t1, :]).then_inc(w2_ld, 16)
            for b in range(B):
                sp.wait_ge(res_ok, b + 1)
                sp.dma_start(of[:, TB * b:TB * b + TB, :], res[:, TB * b:TB * b + TB, :]).then_inc(stored, 16)
            sp.wait_ge(stored, 16 * B)

        @block.gpsimd
        def _(pool):
            steps = [0]

            def then(ins):
                steps[0] += 1
                ins.then_inc(pool_step, 1)
                pool.wait_ge(pool_step, steps[0])

            pool.memset(b1rows[:, :], 0.0).then_inc(b1_clear, 1)
            then(pool.memset(ident[:, :], 0.0))
            then(pool.affine_select(out=ident[:, :], in_=ident[:, :], compare_op=ALU.not_equal, fill=1.0,
                                    base=0, pattern=[[-1, P]], channel_multiplier=1))
            pool.tensor_copy(ident_b[:, :], ident[:, :]).then_inc(ident_ok, 1)
            pool.memset(Qx[:, :, :, R_MAX:HR].bitcast(F32), 0.0).then_inc(pads_ok, 1)
            for i in range(4):
                last = pool.memset(Kd[i][:, :, :].bitcast(F32), 0.0)
            last.then_inc(pads_ok, 1)
            pool.memset(Vx[:, :, :, HD + 1:HR], 0.0).then_inc(pads_ok, 1)
            pool.memset(Vx[:, :, :, HD:HD + 1], 1.0).then_inc(pads_ok, 1)
            for b in range(B):
                pool.wait_ge(hi_ok, 2 * (b + 1))
                rows = slice(TB * b, TB * b + TB)
                q32, k32 = (qk32[:, n].rearrange("p t (h d) -> p t h d", d=HD) for n in range(2))
                pool.tensor_tensor(Qx[:, rows, :, HD:2 * HD], q32, Qx[:, rows, :, 0:HD], ALU.subtract).then_inc(lo_ok, 1)
                pool.tensor_tensor(Kx[:, rows, :, 2 * HD:3 * HD], k32, Kx[:, rows, :, 0:HD], ALU.subtract).then_inc(lo_ok, 1)
            pool.wait_ge(act_step, 2)
            pool.wait_ge(out_w_ld, 64)
            then(pool.tensor_scalar(bout_sb[:, :], bout_sb[:, :], gx[:, 0:1], None, ALU.mult))
            pool.wait_ge(xn_ok, NT)
            pool.tensor_tensor(x_sb[:, :, :], x_sb[:, :, :], bout_sb[:, :].unsqueeze(1).to_broadcast([P, NT, D]),
                               ALU.add).then_inc(xb_ok, 1)
            pool.wait_ge(norm_ok, GROUPS)
            then(pool.memset(hot[:, :], 0.0))
            for part in range(3):
                then(pool.affine_select(out=hot[:, :], in_=hot[:, :], compare_op=ALU.not_equal, fill=1.0,
                                        base=-NE * part, pattern=[[-1, NE]], channel_multiplier=1))
            pool.memset(gates[:, :, NE:NE + NS], 1.0 / NS).then_inc(hot_ok, 1)

            for b in range(B):
                cols = slice(TB * b * P, TB * (b + 1) * P)
                pool.wait_ge(xh_ok, b + 1)
                pool.tensor_tensor(xTl[:, :, cols], xT32[:, :, cols], xTh[:, :, cols], ALU.subtract).then_inc(xl_ok, 1)

            def shared_weights(t):
                k = t % 2
                rows = P if t < SFULL else SREST
                src1 = w1s[:, :, P * t:P * t + rows]
                src2 = w2s[0:rows, t, :]
                if t >= 2:
                    pool.wait_ge(h_mm, 2 * t - 2)
                pool.tensor_copy(w1h[k][:, :, 0:rows], src1).then_inc(ws_hi, 1)
                pool.wait_ge(ws_hi, 2 * t + 1)
                pool.tensor_tensor(w1l[k][:, :, 0:rows], src1, w1h[k][:, :, 0:rows], ALU.subtract).then_inc(ws_ok, 1)
                if t >= 2:
                    pool.wait_ge(y_mm, t - 1)
                pool.tensor_copy(w2h[k][0:rows, :], src2).then_inc(ws_hi, 1)
                pool.wait_ge(ws_hi, 2 * t + 2)
                pool.tensor_tensor(w2l[k][0:rows, :], src2, w2h[k][0:rows, :], ALU.subtract).then_inc(ws_ok, 1)

            def shared_low_part(u):
                t, half = u // 2, u % 2
                rows = P if t < SFULL else SREST
                cols = slice(half * HALF, (half + 1) * HALF)
                pool.wait_ge(hh_ok, u + 1)
                pool.tensor_tensor(hl[t % 2][0:rows, cols], hr[half][0:rows, :], hh[t % 2][0:rows, cols],
                                   ALU.subtract).then_inc(hl_ok, 1)

            pool.wait_ge(ws_ld, 16 * (KD + 2))
            for t in range(2):
                shared_weights(t)
            for t in range(SHT):
                shared_low_part(2 * t)
                shared_low_part(2 * t + 1)
                if t + 2 < SHT:
                    shared_weights(t + 2)
            pool.wait_ge(w1_ld, 16 * 4 * KD)
            pool.wait_ge(w2_ld, 16 * 4)
            with pool.Fori(0, RT // 2) as it:
                for j in range(2):
                    t = it * 2 + (SHT + j)
                    k = (SHT + j) % 2
                    r = it * 2 + j
                    src1 = w1[:, :, bass.ds(r * P, P)]
                    src2 = w2[:, bass.ds(r, 1), :].rearrange("p a n -> p (a n)")
                    pool.wait_ge(h_mm, t * 2 - 2)
                    pool.nop().then_inc(pool_sync, 1)
                    pool.tensor_copy(w1h[k][:, :, :], src1).then_inc(ws_hi, 1)
                    pool.wait_ge(ws_hi, t * 2 + 1)
                    pool.nop().then_inc(pool_sync, 1)
                    pool.tensor_tensor(w1l[k][:, :, :], src1, w1h[k][:, :, :], ALU.subtract).then_inc(ws_ok, 1)
                    pool.wait_ge(y_mm, t - 1)
                    pool.nop().then_inc(pool_sync, 1)
                    pool.tensor_copy(w2h[k][:, :], src2).then_inc(ws_hi, 1)
                    pool.wait_ge(ws_hi, t * 2 + 2)
                    pool.nop().then_inc(pool_sync, 1)
                    pool.tensor_tensor(w2l[k][:, :], src2, w2h[k][:, :], ALU.subtract).then_inc(ws_ok, 1)

        @block.scalar
        def _(act):
            act.dma_start(pos_sb[:, :, :], pos.rearrange("b (t p) a -> p (b t) a", p=P)).then_inc(pos_ld, 16)
            act.dma_start(ctx_sb[:, :, :], ctx.rearrange("b (t p) c -> p (b t) c", p=P)).then_inc(ctx_ld, 16)
            act.dma_start(gx[:, :], rows_to_partitions(g_xattn, P)).then_inc(gate_ld, 16)
            act.dma_start(gf[:, :], rows_to_partitions(g_ffn, P)).then_inc(gate_ld, 16)
            act.wait_ge(ang_ok, 1)
            act.activation(trig[:, :, :, :], ang[:, :, :].rearrange("p s (t f) -> p s t f", f=4), ACT.Sin).then_inc(trig_ok, 1)
            for n, tiles in enumerate((slice(0, TB), slice(TB, NT))):
                act.wait_ge(veps_ok, n + 1)
                act.activation(root[:, tiles], veps[:, tiles], ACT.Sqrt).then_inc(root_ok, 1)
            act.wait_ge(gate_ld, 32)
            act.activation(gx[:, :], gx[:, :], ACT.Tanh).then_inc(act_step, 1)
            act.activation(gf[:, :], gf[:, :], ACT.Tanh).then_inc(act_step, 1)

            def evacuate(b):
                act.wait_ge(xT_mm, b + 1)
                act.activation(xnT[:, b], A_XT[b % 2].rearrange("p (t k q) -> p t k q", t=TB, k=KD), ACT.Copy).then_inc(xT_ok, 1)

            for c in range(2):
                act.wait_ge(cT_mm, c + 1)
                act.activation(ctxT[:, c * NT // 2:(c + 1) * NT // 2, :], A_CT[c].rearrange("p (t q) -> p t q", q=P),
                               ACT.Copy).then_inc(cT_ok, 1)

            def high_parts(b):
                rows = slice(TB * b, TB * b + TB)
                act.wait_ge(kv_mm, TB * (b + 1))
                for t in range(TB):
                    act.activation(Vx[:, TB * b + t, :, 0:HD], A_KV[b % 2][:, t, D:2 * D].rearrange("p (h d) -> p h d", d=HD),
                                   ACT.Copy).then_inc(v_ok, 1)
                q32, k32 = (qk32[:, n].rearrange("p t (h d) -> p t h d", d=HD) for n in range(2))
                act.wait_ge(rot_ok, 2 * b + 1)
                act.activation(Qx[:, rows, :, 0:HD], q32, ACT.Copy).then_inc(hi_ok, 1)
                act.activation(Qx[:, rows, :, 2 * HD:3 * HD], q32, ACT.Copy)
                act.wait_ge(rot_ok, 2 * b + 2)
                act.activation(Kx[:, rows, :, 0:HD], k32, ACT.Copy).then_inc(hi_ok, 1)
                act.activation(Kx[:, rows, :, HD:2 * HD], k32, ACT.Copy).then_inc(qkv_read, 1)

            evacuate(0)
            evacuate(1)
            for k in range(KD):
                act.dma_start(w1s[:, k, :].rearrange("p (e h) -> p e h", h=HID),
                              sw1.rearrange("e (k p) h -> p k e h", p=P)[:, k]).then_inc(ws_ld, 16)
            sflat2 = sw2.rearrange("e h n -> (e h) n")
            act.dma_start(w2s[:, 0:SFULL, :], sflat2[0:SFULL * P, :].rearrange("(t p) n -> p t n", p=P)).then_inc(ws_ld, 16)
            act.dma_start(w2s[0:SREST, SFULL, :], sflat2[SFULL * P:NS * HID, :]).then_inc(ws_ld, 16)
            high_parts(0)
            for b in range(1, B):
                if b + 1 < B:
                    evacuate(b + 1)
                high_parts(b)

            def evacuate_t(i):
                act.wait_ge(t_mm, i + 1)
                if i >= 4:
                    act.wait_ge(s_mm, 4 * (i - 3))
                    act.wait_ge(kd_ld[i % 4], 64 * (i // 4))
                act.activation(QK[i % 4][:, :, :], T_BANK[:, :].rearrange("p (a n) -> p a n", a=2), ACT.Copy).then_inc(t_ok, 1)

            def exponentials(g, n):
                kt, hp = n // 2, n % 2
                if n == 0 and g >= 2:
                    act.wait_ge(pv_mm, 2 * (g - 1))
                act.wait_ge(st_mm, 4 * g + n + 1)
                act.activation(probs[g % 2][:, kt, 2 * hp:2 * hp + 2, :],
                               ST_BANK[(4 * g + n) % 3][:, :].rearrange("p (h q) -> p h q", h=2),
                               ACT.Exp, scale=SCALE).then_inc(exp_ok, 1)

            def step(i):
                g = i - 1
                if 0 <= g < GROUPS:
                    act.wait_ge(t2_mm, g + 1)
                    if g >= 2:
                        act.wait_ge(st_mm, 4 * (g - 1))
                    act.activation(QT[g % 2][:, :], T2_BANK[:, 0:N], ACT.Copy).then_inc(q2_ok, 1)
                if i + 2 < GROUPS:
                    evacuate_t(i + 2)
                if 0 <= g < GROUPS:
                    exponentials(g, 0)
                    exponentials(g, 1)
                if 0 <= i - 2 < GROUPS:
                    act.wait_ge(pv_mm, 2 * (i - 1))
                    if i - 2 >= 2:
                        act.wait_ge(ot_mm, i - 3)
                    act.activation(oT[i % 2][:, :], O_BANK[:, 0:N], ACT.Copy).then_inc(o_ok, 1)
                if 0 <= g < GROUPS:
                    exponentials(g, 2)
                    exponentials(g, 3)

            evacuate_t(0)
            evacuate_t(1)
            for i in range(GROUPS + 3):
                step(i)

            act.wait_ge(norm_ok, GROUPS)
            act.wait_ge(hot_ok, 1)

            def transposed_attention(b):
                act.wait_ge(aT_mm, b + 1)
                if b >= 2:
                    act.wait_ge(pj_mm, b - 1)
                act.activation(attnT[:, b % 2], C_AT[b % 2].rearrange("p (t k q) -> p t k q", t=TB, k=KD),
                               ACT.Copy).then_inc(aT_ok, 1)

            transposed_attention(0)
            for s in range(B + 1):
                if s < B:
                    if s + 1 < B:
                        transposed_attention(s + 1)
                    act.wait_ge(veps_ok, s + 3)
                    rows = slice(TB * s, TB * s + TB)
                    act.activation(root[:, rows], veps[:, rows], ACT.Sqrt).then_inc(root_ok, 1)
                b = s - 1
                if b >= 0:
                    act.wait_ge(x2T_mm, b + 1)
                    cols = slice(TB * b * P, TB * (b + 1) * P)
                    act.activation(xT32[:, :, cols].rearrange("p k (t q) -> p k t q", t=TB),
                                   C_XT[b % 2].rearrange("p (t k q) -> p k t q", t=TB, k=KD),
                                   ACT.Copy).then_inc(x2T_ok, 1)
                    act.wait_ge(x2T_ok, b + 1)
                    act.activation(xTh[:, :, cols], xT32[:, :, cols], ACT.Copy).then_inc(xh_ok, 1)
                if s < B:
                    e = slice(s * NE // B, (s + 1) * NE // B)
                    act.activation(owner[:, :].rearrange("p (e h) -> p e h", h=HID)[:, e, :],
                                   hot[:, e].unsqueeze(2).to_broadcast([3 * NE, NE // B, HID]), ACT.Copy).then_inc(owner_ok, 1)
            act.wait_ge(sub_ok, 1)
            act.activation(pr[:, :, :], lg[:, :, :], ACT.Exp).then_inc(pexp_ok, 1)

            act.wait_ge(b1_ok, 2)

            def relu_static(u):
                t, half = u // 2, u % 2
                rows = P if t < SFULL else SREST
                act.wait_ge(h_mm, u + 1)
                if u >= 2:
                    act.wait_ge(hl_ok, u - 1)
                act.activation(hr[half][0:rows, :], H_BANK[half][0:rows, :], ACT.Relu,
                               bias=b1half[0:rows, t:t + 1], scale=1.0 / NS).then_inc(relu_ok, 1)
                if t >= 2:
                    act.wait_ge(y_mm, t - 1)
                act.wait_ge(relu_ok, u + 1)
                act.activation(hh[t % 2][0:rows, half * HALF:(half + 1) * HALF], hr[half][0:rows, :],
                               ACT.Copy).then_inc(hh_ok, 1)

            for u in range(2 * SHT):
                relu_static(u)
            for half in range(2):
                act.wait_ge(gT_mm, half + 1)
                act.activation(gTf[:, half * HALF:(half + 1) * HALF], G_BANK[half][0:NE + NS, :],
                               ACT.Copy).then_inc(gTf_ok, 1)
            with act.Fori(0, RT // 2) as it:
                for j in range(2):
                    for half in range(2):
                        u = it * 4 + (2 * (SHT + j) + half)
                        act.wait_ge(h_mm, u + 1)
                        act.wait_ge(hl_ok, u - 1)
                        act.nop().then_inc(act_sync, 1)
                        act.activation(hr[half][:, :], H_BANK[half][:, :], ACT.Relu,
                                       bias=b1cols[:, bass.ds(it * 2 + j, 1)]).then_inc(relu_ok, 1)
            act.wait_ge(y_mm, TILES + 1)
            for k in range(KD):
                act.activation(yT[:, k, 0:HALF], Y_BANK[2 * k][:, :], ACT.Copy).then_inc(yT_ok, 1)

        @block.vector
        def _(dve):
            steps = [0]

            def then(ins):
                steps[0] += 1
                ins.then_inc(dve_step, 1)
                dve.wait_ge(dve_step, steps[0])

            TWO_PI = 2 * np.pi
            C1 = float(np.float32(6.28125))
            C2 = float(np.float32(TWO_PI - 6.28125))
            ROUND = float(1.5 * 2 ** 23)
            PI_BELOW = float(np.nextafter(np.float32(np.pi), np.float32(0)))
            FREQ1 = float(np.float32(10000.0) ** np.float32(-0.5))

            dve.wait_ge(pos_ld, 16)
            sine = ang[:, 0].rearrange("p (t a f) -> p t a f", a=2, f=2)
            dve.tensor_scalar(sine[:, :, :, 0], pos_sb[:, :, :], 1.0, None, ALU.mult)
            then(dve.tensor_scalar(sine[:, :, :, 1], pos_sb[:, :, :], FREQ1, None, ALU.mult))
            then(dve.tensor_scalar(ang[:, 1], ang[:, 0], float(np.pi / 2), None, ALU.add))
            then(dve.tensor_scalar(turns[:, :, :], ang[:, :, :], float(1 / TWO_PI), ROUND, ALU.mult, ALU.add))
            then(dve.tensor_scalar(turns[:, :, :], turns[:, :, :], ROUND, None, ALU.subtract))
            then(dve.scalar_tensor_tensor(out=ang[:, :, :], in0=turns[:, :, :], scalar=-C1, in1=ang[:, :, :],
                                          op0=ALU.mult, op1=ALU.add))
            then(dve.scalar_tensor_tensor(out=ang[:, :, :], in0=turns[:, :, :], scalar=-C2, in1=ang[:, :, :],
                                          op0=ALU.mult, op1=ALU.add))
            dve.tensor_scalar(ang[:, :, :], ang[:, :, :], PI_BELOW, -PI_BELOW, ALU.min, ALU.max).then_inc(ang_ok, 1)

            roots = [0]

            def inverse_deviation(first, n):
                rows = slice(first, first + n)
                for t in range(first, first + n):
                    dve.wait_ge(x_ld[t // TB], 16)
                    ins = dve.bn_stats(stats[:, t, :], x_sb[:, t, :])
                then(ins)
                for t in range(first, first + n):
                    ins = dve.bn_aggr(mv[:, t, :], stats[:, t, :])
                then(ins)
                dve.tensor_scalar(veps[:, rows], mv[:, rows, 1], EPS, None, ALU.add).then_inc(veps_ok, 1)
                roots[0] += 1
                dve.wait_ge(root_ok, roots[0])
                then(dve.reciprocal(rstd[:, rows], root[:, rows]))
                then(dve.tensor_tensor(newton[:, rows], rstd[:, rows], rstd[:, rows], ALU.mult))
                then(dve.tensor_tensor(newton[:, rows], newton[:, rows], veps[:, rows], ALU.mult))
                then(dve.tensor_scalar(newton[:, rows], newton[:, rows], -0.5, 1.5, ALU.mult, ALU.add))
                then(dve.tensor_tensor(rstd[:, rows], rstd[:, rows], newton[:, rows], ALU.mult))

            def normalise_rows(b, dst, done):
                for t in range(TB):
                    n = TB * b + t
                    dve.tensor_scalar(dst[:, t, :], x_sb[:, n, :], mv[:, n, 0:1], rstd[:, n:n + 1],
                                      ALU.subtract, ALU.mult).then_inc(done, 1)

            def rotate(b, n, psum):
                rows = slice(TB * b, TB * b + TB)
                c8, s8 = (v[:, rows].rearrange("p t f c -> p t (f c)").unsqueeze(2).to_broadcast([P, TB, H, 8])
                          for v in (cos8, sin8))
                src = psum.rearrange("p t (h d) -> p t h d", d=HD)
                t1, t2 = (v[:, :, :].rearrange("p t (h d) -> p t h d", d=HD) for v in (rot1, rot2))
                if 2 * b + n:
                    dve.wait_ge(rot_ok, 2 * b + n)
                dve.tensor_tensor(t1, src, c8, ALU.mult)
                then(dve.tensor_tensor(t2, src, s8, ALU.mult))
                pairs = [v.rearrange("p t (m c) -> p (t m) c", c=2) for v in (rot1[:, :, :], rot2[:, :, :], qk32[:, n])]
                if b:
                    dve.wait_ge(qkv_read, b)
                    dve.wait_ge(lo_ok, 2 * b)
                dve.tensor_tensor(pairs[2][:, :, 0], pairs[0][:, :, 0], pairs[1][:, :, 1], ALU.add)
                dve.tensor_tensor(pairs[2][:, :, 1], pairs[0][:, :, 1], pairs[1][:, :, 0], ALU.add).then_inc(rot_ok, 1)

            inverse_deviation(0, TB)
            normalise_rows(0, xn[:, 0], xn_ok)
            inverse_deviation(TB, NT - TB)
            for b in range(1, B):
                normalise_rows(b, xn[:, b], xn_ok)
            dve.memset(Kx[:, :, :, R_MAX:R_MAX + 2].bitcast(F32), 1.0)
            dve.memset(Kx[:, :, :, R_MAX + 2:HR].bitcast(F32), 0.0).then_inc(pads_ok, 1)
            dve.wait_ge(trig_ok, 1)
            dve.tensor_copy(cos8[:, :, :, :], trig[:, 1].unsqueeze(3).to_broadcast([P, NT, 4, 2]))
            dve.tensor_copy(sin8[:, :, :, 0], trig[:, 0])
            then(dve.tensor_scalar(sin8[:, :, :, 1], trig[:, 0], -1.0, None, ALU.mult))
            for b in range(B):
                dve.wait_ge(q_mm, b + 1)
                rotate(b, 0, A_Q[b % 2].rearrange("p (t n) -> p t n", t=TB))
                dve.wait_ge(v_ok, TB * (b + 1))
                rotate(b, 1, A_KV[b % 2][:, :, 0:D])
            dve.wait_ge(b1_mm, 1)
            dve.tensor_copy(b1cols[:, :], A_B1[:, 0:TILES]).then_inc(b1_ok, 1)
            dve.tensor_scalar(b1half[:, :], A_B1[:, SB_ROW:TILES], 1.0 / NS, None, ALU.mult).then_inc(b1_ok, 1)

            def row_max(i, n):
                qt, hp = n // 2, n % 2
                if n == 0 and i >= 2:
                    dve.wait_ge(m_ok, i - 1)
                dve.wait_ge(s_mm, 4 * i + n + 1)
                dve.tensor_reduce(nmax[i % 2][:, qt, 2 * hp:2 * hp + 2],
                                  S_BANK[n % 2][:, :].rearrange("p (h k) -> p h k", h=2),
                                  AX.X, ALU.max, negate=True).then_inc(s_max, 1)

            def normalise(i):
                b, g = i // NG, i % NG
                o = T2_BANK[:, 0:TB * P].rearrange("p (t h c) -> p t h c", t=TB, h=GH)
                if i >= 2:
                    dve.wait_ge(norm_ok, i - 1)
                dve.wait_ge(ot_mm, i + 1)
                dve.reciprocal(rden[i % 2][:, :, :], o[:, :, :, HD]).then_inc(rd_ok, 1)
                dve.wait_ge(rd_ok, i + 1)
                dst = attn[:, TB * b:TB * b + TB, GH * HD * g:GH * HD * (g + 1)].rearrange("p t (h d) -> p t h d", d=HD)
                dve.tensor_tensor(dst, o[:, :, :, 0:HD],
                                  rden[i % 2][:, :, :].unsqueeze(3).to_broadcast([P, TB, GH, HD]),
                                  ALU.mult).then_inc(norm_ok, 1)

            for i in range(GROUPS + 3):
                if i < GROUPS:
                    row_max(i, 0)
                    row_max(i, 1)
                    row_max(i, 2)
                if 0 <= i - 3:
                    normalise(i - 3)
                if i < GROUPS:
                    row_max(i, 3)
                    b, g = i // NG, i % NG
                    dst = Qx[:, TB * b:TB * b + TB, GH * g:GH * g + GH, :]
                    dve.wait_ge(s_max, 4 * i + 4)
                    dve.tensor_copy(dst[:, :, :, R_MAX], nmax[i % 2][:, :, :]).then_inc(mhi_ok, 1)
                    dve.wait_ge(mhi_ok, i + 1)
                    dve.tensor_tensor(dst[:, :, :, R_MAX + 1], nmax[i % 2][:, :, :], dst[:, :, :, R_MAX],
                                      ALU.subtract).then_inc(m_ok, 1)

            dve.wait_ge(act_step, 2)
            dve.wait_ge(xb_ok, 1)
            for s in range(B + 2):
                if s < B:
                    rows = slice(TB * s, TB * s + TB)
                    dve.wait_ge(pj_mm, s + 1)
                    dve.scalar_tensor_tensor(out=x_sb[:, rows, :], in0=C_PJ[s % 2].rearrange("p (t n) -> p t n", t=TB),
                                             scalar=gx[:, 0:1], in1=x_sb[:, rows, :],
                                             op0=ALU.mult, op1=ALU.add).then_inc(pj_ok, 1)
                    dve.wait_ge(pj_ok, s + 1)
                    if s >= 2:
                        dve.wait_ge(x2T_mm, s - 1)
                    inverse_deviation(TB * s, TB)
                    normalise_rows(s, xn2[:, s % 2], xn2_ok)
                b = s - 2
                if b >= 0:
                    dve.wait_ge(rt_mm, b + 1)
                    dve.tensor_tensor(lg[:, TB * b:TB * b + TB, :],
                                      C_RT[:, 0:TB * NE].rearrange("p (t e) -> p t e", t=TB),
                                      rtb_sb[:, :].unsqueeze(1).to_broadcast([P, TB, NE]), ALU.add).then_inc(lg_ok, 1)

            def per_expert(v):
                return v.unsqueeze(2).to_broadcast([P, NT, NE])

            dve.wait_ge(lg_ok, B)
            then(dve.tensor_reduce(red[:, 0], lg[:, :, :], AX.X, ALU.max))
            dve.tensor_tensor(lg[:, :, :], lg[:, :, :], per_expert(red[:, 0]), ALU.subtract).then_inc(sub_ok, 1)
            for c in cum:
                dve.memset(c[:, :, 0:PAD], 0.0)
            dve.wait_ge(pexp_ok, 1)
            then(dve.tensor_reduce(red[:, 1], pr[:, :, :], AX.X, ALU.add))
            then(dve.reciprocal(red[:, 2], red[:, 1]))
            then(dve.tensor_tensor(pr[:, :, :], pr[:, :, :], per_expert(red[:, 2]), ALU.mult))
            for t in range(NT):
                ins = dve.max(top8[:, t, :], pr[:, t, :])
            then(ins)
            sixth = per_expert(top8[:, :, TOPK - 1])
            then(dve.tensor_tensor(gt[:, :, :], pr[:, :, :], sixth, ALU.is_gt))
            dve.tensor_reduce(red[:, 3], gt[:, :, :], AX.X, ALU.add)
            dve.tensor_tensor(eq[:, :, :], pr[:, :, :], sixth, ALU.is_equal)
            then(dve.tensor_tensor(cum[0][:, :, PAD:], pr[:, :, :], sixth, ALU.is_equal))
            then(dve.tensor_scalar(red[:, 0], red[:, 3], -1.0, float(TOPK), ALU.mult, ALU.add))
            shift, a = 1, 0
            while shift < NE:
                then(dve.tensor_tensor(cum[1 - a][:, :, PAD:], cum[a][:, :, PAD:],
                                       cum[a][:, :, PAD - shift:PAD + NE - shift], ALU.add))
                shift, a = 2 * shift, 1 - a
            then(dve.tensor_tensor(sel[:, :, :], cum[a][:, :, PAD:], per_expert(red[:, 0]), ALU.is_le))
            then(dve.tensor_tensor(eq[:, :, :], eq[:, :, :], sel[:, :, :], ALU.mult))
            then(dve.tensor_tensor(gt[:, :, :], gt[:, :, :], eq[:, :, :], ALU.add))
            then(dve.tensor_tensor(sel[:, :, :], gt[:, :, :], pr[:, :, :], ALU.mult))
            then(dve.tensor_reduce(red[:, 1], sel[:, :, :], AX.X, ALU.add))
            then(dve.reciprocal(red[:, 2], red[:, 1]))
            dve.wait_ge(hot_ok, 1)
            then(dve.tensor_tensor(gates[:, :, 0:NE], sel[:, :, :], per_expert(red[:, 2]), ALU.mult))
            then(dve.tensor_copy(gparts[:, :, 0, :], gates[:, :, 0:NE]))
            then(dve.tensor_tensor(sel[:, :, :], gates[:, :, 0:NE], gparts[:, :, 0, :], ALU.subtract))
            then(dve.tensor_copy(gparts[:, :, 1, :], sel[:, :, :]))
            then(dve.tensor_tensor(sel[:, :, :], sel[:, :, :], gparts[:, :, 1, :], ALU.subtract))
            dve.tensor_copy(gparts[:, :, 2, :], sel[:, :, :]).then_inc(gparts_ok, 1)

            dve.wait_ge(gT_mm, 3)
            dve.tensor_copy(gT3[:, :], G_BANK[0].bitcast(BF16)[0:3 * NE, :]).then_inc(gT3_ok, 1)
            with dve.Fori(0, RT // 2) as it:
                for j in range(2):
                    for half in range(2):
                        tt = SHT + j
                        u = it * 4 + (2 * tt + half)
                        r = it * 4 + (2 * j + half)
                        cols = slice(half * HALF, (half + 1) * HALF)
                        dve.wait_ge(hl_ok, u - 1)
                        dve.wait_ge(g_mm, r + 1)
                        dve.wait_ge(relu_ok, u + 1)
                        dve.tensor_tensor(hg[half][:, :], hr[half][:, :], G_BANK[half][:, :], ALU.mult).then_inc(hg_ok, 1)
                        dve.wait_ge(y_mm, it * 2 + (tt - 1))
                        dve.wait_ge(hg_ok, r + 1)
                        dve.tensor_copy(hh[tt % 2][:, cols], hg[half][:, :]).then_inc(hh_ok, 1)
                        dve.wait_ge(hh_ok, u + 1)
                        dve.tensor_tensor(hl[tt % 2][:, cols], hg[half][:, :], hh[tt % 2][:, cols],
                                          ALU.subtract).then_inc(hl_ok, 1)
            dve.wait_ge(y_mm, TILES + 1)
            for k in range(KD):
                dve.tensor_copy(yT[:, k, HALF:TOK], Y_BANK[2 * k + 1][:, :]).then_inc(yT_ok, 1)
            for b in range(B):
                rows = slice(TB * b, TB * b + TB)
                dve.wait_ge(yb_mm, b + 1)
                dve.scalar_tensor_tensor(out=res[:, rows, :], in0=E_BANK[b].rearrange("p (t n) -> p t n", t=TB),
                                         scalar=gf[:, 0:1], in1=x_sb[:, rows, :],
                                         op0=ALU.mult, op1=ALU.add).then_inc(res_ok, 1)

        @block.tensor
        def _(pe):
            pe.wait_ge(ident_ok, 1)
            pe.wait_ge(ctx_ld, 16)
            for c in range(2):
                for t in range(NT // 2):
                    ins = pe.transpose(A_CT[c][:, t * P:(t + 1) * P], ctx_sb[:, c * NT // 2 + t, :], ident[:, :])
                ins.then_inc(cT_mm, 1)

            def transposed_rows(b):
                pe.wait_ge(xn_ok, TB * (b + 1))
                if b >= 2:
                    pe.wait_ge(xT_ok, b - 1)
                for t in range(TB):
                    for k in range(KD):
                        n = (t * KD + k) * P
                        ins = pe.transpose(A_XT[b % 2][:, n:n + P], xn[:, b, t, k * P:(k + 1) * P], ident[:, :])
                ins.then_inc(xT_mm, 1)

            def projections(b):
                pe.wait_ge(cT_ok, 2)
                pe.wait_ge(wkv_ld, 16)
                if b >= 2:
                    pe.wait_ge(rot_ok, 2 * (b - 1))
                    pe.wait_ge(v_ok, TB * (b - 1))
                for t in range(TB):
                    pe.matmul(A_KV[b % 2][:, t, :], ctxT[:, TB * b + t, :], wkv_sb[:, :], start=True, stop=True).then_inc(kv_mm, 1)
                pe.wait_ge(xT_ok, b + 1)
                pe.wait_ge(wq_ld, 16)
                for t in range(TB):
                    for k in range(KD):
                        ins = pe.matmul(A_Q[b % 2][:, t * D:(t + 1) * D], xnT[:, b, t, k, :], wq_sb[:, k, :],
                                        start=(k == 0), stop=(k == KD - 1))
                ins.then_inc(q_mm, 1)

            transposed_rows(0)
            transposed_rows(1)
            for b in range(B):
                projections(b)
                if b + 2 < B:
                    transposed_rows(b + 2)
            pe.wait_ge(bias_ld, 48)
            pe.transpose(A_B1[:, 0:TILES], b1rows[:, :], ident[0:TILES, 0:TILES]).then_inc(b1_mm, 1)

            def transposes(i):
                b, g = i // NG, i % NG
                if g == 0:
                    pe.wait_ge(qkv_read, b + 1)
                    pe.wait_ge(lo_ok, 2 * (b + 1))
                if i:
                    pe.wait_ge(t_ok, i)
                for a, src in enumerate((Qx, Kx)):
                    for t in range(TB):
                        n = (a * TB + t) * P
                        ins = pe.transpose(T_BANK[:, n:n + P],
                                           src[:, TB * b + t, GH * g:GH * g + GH, :].rearrange("p h r -> p (h r)").bitcast(F32),
                                           ident[:, :])
                ins.then_inc(t_mm, 1)

            def scores(i, n):
                qt, hp = n // 2, n % 2
                if n == 0:
                    pe.wait_ge(kd_ld[i % 4], 64 * (i // 4 + 1))
                    pe.wait_ge(t_ok, i + 1)
                if 4 * i + n >= 2:
                    pe.wait_ge(s_max, 4 * i + n - 1)
                pe.matmul(S_BANK[n % 2], QK[i % 4][:, 0, qt * P:(qt + 1) * P], Kd[i % 4][:, 2 * hp:2 * hp + 2, :],
                          start=True, stop=True).then_inc(s_mm, 1)

            def transposes_with_max(i):
                b, g = i // NG, i % NG
                pe.wait_ge(m_ok, i + 1)
                if i >= 3:
                    pe.wait_ge(norm_ok, i - 2)
                for t in range(TB):
                    ins = pe.transpose(T2_BANK[:, t * P:(t + 1) * P],
                                       Qx[:, TB * b + t, GH * g:GH * g + GH, :].rearrange("p h r -> p (h r)").bitcast(F32),
                                       ident[:, :])
                ins.then_inc(t2_mm, 1)

            def shifted_scores(i, n):
                kt, hp = n // 2, n % 2
                if n == 0:
                    pe.wait_ge(q2_ok, i + 1)
                if 4 * i + n >= 3:
                    pe.wait_ge(exp_ok, 4 * i + n - 2)
                for h in range(2):
                    ins = pe.matmul(ST_BANK[(4 * i + n) % 3][:, h * N:(h + 1) * N],
                                    Kd[i % 4][:, 2 * hp + h, kt * P:(kt + 1) * P], QT[i % 2][:, :], start=True, stop=True)
                ins.then_inc(st_mm, 1)

            def values(i, kt):
                b, g = i // NG, i % NG
                pe.wait_ge(exp_ok, 4 * i + 2 * (kt + 1))
                if kt == 0 and i:
                    pe.wait_ge(o_ok, i)
                for h in range(GH):
                    ins = pe.matmul(O_BANK[HR * h:HR * h + HR, 0:N], Vx[:, TB * b + kt, GH * g + h, :],
                                    probs[i % 2][:, kt, h, :], start=(kt == 0), stop=(kt == TB - 1))
                ins.then_inc(pv_mm, 1)

            def outputs(i):
                pe.wait_ge(o_ok, i + 1)
                pe.wait_ge(q2_ok, min(i + 3, GROUPS))
                if i:
                    pe.wait_ge(norm_ok, i)
                for t in range(TB):
                    ins = pe.transpose(T2_BANK[:, t * P:(t + 1) * P], oT[i % 2][:, t * P:(t + 1) * P], ident[:, :])
                ins.then_inc(ot_mm, 1)

            transposes(0)
            transposes(1)
            pe.wait_ge(pads_ok, 5)
            pe.wait_ge(rot_ok, 2 * B)
            pe.wait_ge(v_ok, NT)
            pe.wait_ge(b1_ok, 2)
            for i in range(GROUPS + 3):
                new, shifted, weighted = i < GROUPS, 0 <= i - 1 < GROUPS, 0 <= i - 2 < GROUPS
                if new:
                    scores(i, 0)
                    scores(i, 1)
                if weighted:
                    values(i - 2, 0)
                if shifted:
                    transposes_with_max(i - 1)
                if i + 2 < GROUPS:
                    transposes(i + 2)
                if new:
                    scores(i, 2)
                if i >= 3:
                    outputs(i - 3)
                if shifted:
                    shifted_scores(i - 1, 0)
                    shifted_scores(i - 1, 1)
                if new:
                    scores(i, 3)
                if weighted:
                    values(i - 2, 1)
                if shifted:
                    shifted_scores(i - 1, 2)
                    shifted_scores(i - 1, 3)

            pe.wait_ge(norm_ok, GROUPS)
            pe.wait_ge(out_w_ld, 64)

            def attention_transposed(b):
                if b >= 2:
                    pe.wait_ge(aT_ok, b - 1)
                for t in range(TB):
                    for k in range(KD):
                        n = (t * KD + k) * P
                        ins = pe.transpose(C_AT[b % 2][:, n:n + P], attn[:, TB * b + t, k * P:(k + 1) * P], ident[:, :])
                ins.then_inc(aT_mm, 1)

            def output_projection(b):
                pe.wait_ge(aT_ok, b + 1)
                if b >= 2:
                    pe.wait_ge(pj_ok, b - 1)
                for t in range(TB):
                    for k in range(KD):
                        ins = pe.matmul(C_PJ[b % 2][:, t * D:(t + 1) * D], attnT[:, b % 2, t, k, :], wout_sb[:, k, :],
                                        start=(k == 0), stop=(k == KD - 1))
                ins.then_inc(pj_mm, 1)

            def second_rows_transposed(b):
                pe.wait_ge(xn2_ok, TB * (b + 1))
                if b >= 2:
                    pe.wait_ge(x2T_ok, b - 1)
                for t in range(TB):
                    for k in range(KD):
                        n = (t * KD + k) * P
                        ins = pe.transpose(C_XT[b % 2][:, n:n + P], xn2[:, b % 2, t, k * P:(k + 1) * P], ident[:, :])
                ins.then_inc(x2T_mm, 1)

            def router_scores(b):
                pe.wait_ge(x2T_ok, b + 1)
                if b:
                    pe.wait_ge(lg_ok, b)
                for t in range(TB):
                    for k in range(KD):
                        n = (TB * b + t) * P
                        ins = pe.matmul(C_RT[:, t * NE:(t + 1) * NE], xT32[:, k, n:n + P], rtw_sb[:, k, :],
                                        start=(k == 0), stop=(k == KD - 1))
                ins.then_inc(rt_mm, 1)

            attention_transposed(0)
            attention_transposed(1)
            output_projection(0)
            for s in range(B):
                if s + 2 < B:
                    attention_transposed(s + 2)
                if s + 1 < B:
                    output_projection(s + 1)
                second_rows_transposed(s)
                if s:
                    router_scores(s - 1)
            router_scores(B - 1)

            def hidden(t, k2, rows, r=None):
                for half in range(2):
                    u = t * 2 + half
                    if not isinstance(t, int) or t:
                        pe.wait_ge(relu_ok, u - 1)
                        pe.wait_ge(hl_ok, u - 1)
                    pe.wait_ge(ws_ok, t * 2 + 1)
                    cols = slice(half * HALF, (half + 1) * HALF)
                    parts = [(w, v, k) for w, v in ((w1h, xTh), (w1l, xTh), (w1h, xTl)) for k in range(KD)]
                    for n, (w, v, k) in enumerate(parts):
                        ins = pe.matmul(H_BANK[half][0:rows, :], w[k2][:, k, 0:rows], v[:, k, cols],
                                        start=(n == 0), stop=(n == len(parts) - 1))
                    ins.then_inc(h_mm, 1)
                    if r is not None:
                        pe.matmul(G_BANK[half], owner[:, bass.ds(r * P, P)], gT3[:, cols],
                                  start=True, stop=True).then_inc(g_mm, 1)

            def result(t, k2, rows, first=False):
                pe.wait_ge(ws_ok, t * 2 + 2)
                for half in range(2):
                    pe.wait_ge(hl_ok, t * 2 + half + 1)
                    cols = slice(half * HALF, (half + 1) * HALF)
                    for k in range(KD):
                        wc = slice(k * P, (k + 1) * P)
                        for n, (w, v) in enumerate(((w2h, hh), (w2l, hh), (w2h, hl))):
                            ins = pe.matmul(Y_BANK[2 * k + half], w[k2][0:rows, wc], v[k2][0:rows, cols],
                                            start=(first and n == 0), stop=False, skip_group_check=True)
                ins.then_inc(y_mm, 1)

            pe.wait_ge(xh_ok, B)
            pe.wait_ge(xl_ok, B)
            hidden(0, 0, P)
            pe.wait_ge(lg_ok, B)
            for t in range(SHT - 1):
                hidden(t + 1, (t + 1) % 2, P if t + 1 < SFULL else SREST)
                result(t, t % 2, P, first=(t == 0))
            pe.wait_ge(gparts_ok, 1)
            for half in range(2):
                for c in range(NT // 2):
                    t = half * (NT // 2) + c
                    ins = pe.transpose(G_BANK[half][0:NE + NS, c * P:(c + 1) * P], gates[:, t, :], ident[:, :])
                ins.then_inc(gT_mm, 1)
            pe.wait_ge(gTf_ok, 1)
            for t in range(NT):
                ins = pe.transpose(G_BANK[0].bitcast(BF16)[0:3 * NE, t * P:(t + 1) * P],
                                   gparts[:, t].rearrange("p a e -> p (a e)"), ident_b[:, :])
            ins.then_inc(gT_mm, 1)
            pe.wait_ge(gTf_ok, 2)
            pe.wait_ge(gT3_ok, 1)
            pe.wait_ge(owner_ok, B)
            hidden(SHT, SHT % 2, P, r=0)
            result(SHT - 1, (SHT - 1) % 2, SREST)
            with pe.Fori(0, RT // 2 - 1) as it:
                for j in range(2):
                    t = it * 2 + (SHT + j)
                    hidden(t + 1, (SHT + j + 1) % 2, P, r=it * 2 + (j + 1))
                    result(t, (SHT + j) % 2, P)
            hidden(TILES - 1, (TILES - 1) % 2, P, r=RT - 1)
            result(TILES - 2, (TILES - 2) % 2, P)
            result(TILES - 1, (TILES - 1) % 2, P)
            pe.wait_ge(b2_ld, 32)
            for k in range(KD):
                for half in range(2):
                    ins = pe.matmul(Y_BANK[2 * k + half], b2_sb[:, k * P:(k + 1) * P],
                                    gTf[:, half * HALF:(half + 1) * HALF], start=False, stop=True, skip_group_check=True)
            ins.then_inc(y_mm, 1)
            for b in range(B):
                pe.wait_ge(yT_ok, 4)
                for t in range(TB):
                    for k in range(KD):
                        n = (TB * b + t) * P
                        ins = pe.transpose(E_BANK[b][:, (t * KD + k) * P:(t * KD + k + 1) * P],
                                           yT[:, k, n:n + P], ident[:, :])
                ins.then_inc(yb_mm, 1)


_INS = ['x', 'ctx_1024', 'fside_BxSx2_0', 'g_xattn', 'g_ffn', 'L0_xattn_Wq', 'L0_xattn_Wkv', 'L0_xattn_Wout',
        'L0_xattn_bout', 'L0_ffn_sw1', 'L0_ffn_sb1', 'L0_ffn_sw2', 'L0_ffn_sb2', 'L0_ffn_rw1', 'L0_ffn_rb1',
        'L0_ffn_rw2', 'L0_ffn_rb2', 'L0_ffn_router_w', 'L0_ffn_router_b']
_OUTS = [((4, 256, 256), 'float32')]


def kernel(**inputs):
    import numpy as _np
    import concourse.bacc as _bacc
    from concourse import mybir as _mybir
    from concourse.bass_utils import run_bass_kernel_spmd as _run

    nc = _bacc.Bacc("TRN2", target_bir_lowering=False, num_devices=1)
    arrays, args = {}, []
    for name in _INS:
        a = _np.ascontiguousarray(inputs[name])
        arrays[f"in_{name}_dram"] = a
        args.append(nc.dram_tensor(f"in_{name}_dram", a.shape, _mybir.dt.from_np(a.dtype), kind="ExternalInput").ap())
    for i, (shape, dtype) in enumerate(_OUTS):
        dt = _mybir.dt.from_np(_np.dtype(dtype))
        args.append(nc.dram_tensor(f"out_{i}_dram", shape, dt, kind="ExternalOutput").ap())
    gated_cross_attention_moe(nc, *args)
    r = _run(nc, [arrays], core_ids=[0])
    got = tuple(r.results[0][f"out_{i}_dram"] for i in range(len(_OUTS)))
    return got[0]
```

```python
from contextlib import ExitStack

import numpy as np

import concourse.bass as bass
from concourse import mybir

ALU = mybir.AluOpType
ACT = mybir.ActivationFunctionType
AX = mybir.AxisListType
F32 = mybir.dt.float32
F32R = mybir.dt.float32r
BF16 = mybir.dt.bfloat16

P = 128
WARM_UP, WARM_START = 14, 8
BANK = 512


def gated_cross_attention_moe(
    nc, x, ctx, pos, g_xattn, g_ffn, wq, wkv, wout, bout,
    sw1, sb1, sw2, sb2, rw1, rb1, rw2, rb2, router_w, router_b, out,
):
    B, N, D = x.shape
    C = ctx.shape[2]
    HD = 8
    H = D // HD
    NT = B * N // P
    TB = N // P
    KD = D // P
    GH = 4
    HR = P // GH
    NG = H // GH
    GROUPS = B * NG
    PAIRS = GROUPS // 2
    SLOT = HR // 2
    TOK = B * N
    HALF = TOK // 2
    SCALE = float(1.0 / np.sqrt(np.float32(HD)))
    EPS = 1e-5
    NS, _, HID = sw1.shape
    NE = rw1.shape[0]
    TOPK = 6
    RT = NE * HID // P
    assert RT * P == NE * HID and HALF == BANK and C == P
    SFULL, SREST = divmod(NS * HID, P)
    SHT = SFULL + 1
    TILES = SHT + RT
    RING = 5
    AHEAD = RING - 2
    SB_ROW = RT

    R_MAX = 3 * HD

    with ExitStack() as keep:
        def sb(name, shape, dt=F32, where=keep):
            return where.enter_context(nc.sbuf_tensor(name, shape, dt))

        def sem(name):
            return keep.enter_context(nc.semaphore(name))

        x_sb = sb("x_sb", [P, NT, D])
        gx = sb("gx", [P, 1])
        gf = sb("gf", [P, 1])
        ident = sb("ident", [P, P])
        ident_b = sb("ident_b", [P, P], BF16)
        stats = sb("stats", [P, NT, 6])
        mv = sb("mv", [P, NT, 2])
        veps = sb("veps", [P, NT])
        root = sb("root", [P, NT])
        rstd = sb("rstd", [P, NT])
        newton = sb("newton", [P, NT])
        wout_sb = sb("wout_sb", [P, KD, D])
        bout_sb = sb("bout_sb", [P, D])
        rtw_sb = sb("rtw_sb", [P, KD, NE])
        rtb_sb = sb("rtb_sb", [P, NE])
        b1rows = sb("b1rows", [TILES, P])
        b1cols = sb("b1cols", [P, TILES])
        b1half = sb("b1half", [P, SHT])
        b2_sb = sb("b2_sb", [NE + NS, D])
        attn = sb("attn", [P, NT, D])
        w1s = sb("w1s", [P, KD, NS * HID])
        w2s = sb("w2s", [P, SHT, D])

        early = ExitStack()
        def sa(name, shape, dt=F32):
            return sb(name, shape, dt, early)
        wq_sb = sa("wq_sb", [P, KD, D])
        wkv_sb = sa("wkv_sb", [P, 2 * D])
        ctx_sb = sa("ctx_sb", [P, NT, C])
        pos_sb = sa("pos_sb", [P, NT, 2])
        ang = sa("ang", [P, 2, NT * 4])
        turns = sa("turns", [P, 2, NT * 4])
        trig = sa("trig", [P, 2, NT, 4])
        cos8 = sa("cos8", [P, NT, 4, 2])
        sin8 = sa("sin8", [P, NT, 4, 2])
        xn = sa("xn", [P, B, TB, D])
        xnT = sa("xnT", [P, B, TB, KD, P])
        ctxT = sa("ctxT", [P, NT, P])
        qk32 = [sa(f"qk32{i}", [P, 2, TB, D]) for i in range(2)]
        Qx = sa("Qx", [P, NT, H, HR], F32R)
        Kx = sa("Kx", [P, NT, H, HR], F32R)
        Vx = sa("Vx", [P, NT, H, HR])
        QK = [sa(f"QK{i}", [P, 2, N], F32R) for i in range(RING - 1)]
        Kd = [sa(f"Kd{i}", [P, GH, N], F32R) for i in range(RING - 1)]
        QT = [sa(f"QT{i}", [P, N], F32R) for i in range(2)]
        nmax = [sa(f"nmax{i}", [P, TB, GH]) for i in range(2)]
        probs = [sa(f"probs{i}", [P, TB, GH, N]) for i in range(2)]
        oT = [sa(f"oT{i}", [P, N]) for i in range(2)]
        rden = [sa(f"rden{i}", [P, TB, 2, GH]) for i in range(2)]
        Vpairs = Vx[:, :, :, :].rearrange("p n (m s h) r -> p n m s h r", s=2, h=GH)
        attnT = Vx[:, 3].rearrange("p h r -> p (h r)").rearrange("p (b t k q) -> p b t k q", b=2, t=TB, k=KD)
        xn2 = Vx[:, 4:6].rearrange("p a h r -> p (a h r)").rearrange("p (b t d) -> p b t d", b=B, t=TB)
        turned = [v[:, :, :, :].rearrange("p t h n -> p (t h n)").rearrange("p (n s t c) -> p n s t c", n=2, s=2, t=TB)
                  for v in probs]
        early.close()

        w1h = [sb(f"w1h{i}", [P, KD, P], F32R) for i in range(3)]
        w1l = [sb(f"w1l{i}", [P, KD, P], F32R) for i in range(3)]
        w2h = [sb(f"w2h{i}", [P, D], F32R) for i in range(3)]
        w2l = [sb(f"w2l{i}", [P, D], F32R) for i in range(3)]
        hot = sb("hot", [3 * NE, NE], BF16)
        owner = sb("owner", [3 * NE, RT * P], BF16)

        ring_end = ExitStack()
        QK.append(sb("QK_last", [P, 2, N], F32R, ring_end))
        Kd.append(sb("Kd_last", [P, GH, N], F32R, ring_end))
        ring_end.close()

        w1 = sb("w1", [P, KD, NE * HID])
        w2 = sb("w2", [P, RT, D])
        hr = [sb(f"hr{i}", [P, HALF]) for i in range(2)]
        hg = [sb(f"hg{i}", [P, HALF]) for i in range(2)]
        hh = [sb(f"hh{i}", [P, TOK], F32R) for i in range(2)]
        hl = [sb(f"hl{i}", [P, TOK], F32R) for i in range(2)]
        xT32 = sb("xT32", [P, KD, TOK])
        xTh = sb("xTh", [P, KD, TOK], F32R)
        xTl = sb("xTl", [P, KD, TOK], F32R)
        lg, pr, gt, eq, sel = (sb(n, [P, NT, NE]) for n in ("lg", "pr", "gt", "eq", "sel"))
        lgT = sb("lgT", [P, N])
        PAD = NE // 2
        cum = [sb(f"cum{i}", [P, NT, PAD + NE]) for i in range(2)]
        top8 = sb("top8", [P, NT, 8])
        red = sb("red", [P, 4, NT])
        gates = sb("gates", [P, NT, NE + NS])
        gparts = sb("gparts", [P, NT, 3, NE], BF16)
        gTf = sb("gTf", [NE + NS, TOK])
        gT3 = sb("gT3", [3 * NE, TOK], BF16)
        yT = xT32
        res = attn

        psum = keep.enter_context(nc.psum_tensor("psum", [P, 8, BANK], F32))
        banks = [psum[:, i, :] for i in range(8)]

        x_ld = [sem(f"x_ld{b}") for b in range(B)]
        w_ld = [sem(f"w_ld{c}") for c in range(2)]
        pos_ld, ctx_ld, wq_ld, wkv_ld, gate_ld, out_w_ld, bias_ld, b2_ld = (
            sem(n) for n in ("pos_ld", "ctx_ld", "wq_ld", "wkv_ld", "gate_ld", "out_w_ld", "bias_ld", "b2_ld"))
        ws_ld = sem("ws_ld")
        warm = sem("warm")
        turn_mul = sem("turn_mul")
        lgT_mm, lgT_ok = sem("lgT_mm"), sem("lgT_ok")
        b1_clear, ident_ok, pads_ok, pool_step = sem("b1_clear"), sem("ident_ok"), sem("pads_ok"), sem("pool_step")
        kd_clear, v_pads_ok = sem("kd_clear"), sem("v_pads_ok")
        dve_step, act_step = sem("dve_step"), sem("act_step")
        veps_ok, root_ok = sem("veps_ok"), sem("root_ok")
        ang_ok, trig_ok, xn_ok, xT_mm, xT_ok, cT_mm, cT_ok = (
            sem(n) for n in ("ang_ok", "trig_ok", "xn_ok", "xT_mm", "xT_ok", "cT_mm", "cT_ok"))
        q_mm, kv_mm, rot_ok, qkv_read, hi_ok, lo_ok, v_ok = (
            sem(n) for n in ("q_mm", "kv_mm", "rot_ok", "qkv_read", "hi_ok", "lo_ok", "v_ok"))
        t_mm, t_ok, s_mm, s_max, mhi_ok, m_ok, t2_mm, q2_ok, st_mm, exp_ok, pv_mm, o_ok, ot_mm, rd_ok, norm_ok = (
            sem(n) for n in ("t_mm", "t_ok", "s_mm", "s_max", "mhi_ok", "m_ok", "t2_mm", "q2_ok",
                             "st_mm", "exp_ok", "pv_mm", "o_ok", "ot_mm", "rd_ok", "norm_ok"))
        kd_ld = [sem(f"kd_ld{i}") for i in range(RING)]
        aT_mm, aT_ok, pj_mm, xn2_ok, x2T_mm, x2T_ok, rt_mm, lg_ok, pj_ok, xb_ok = (
            sem(n) for n in ("aT_mm", "aT_ok", "pj_mm", "xn2_ok", "x2T_mm", "x2T_ok", "rt_mm", "lg_ok", "pj_ok", "xb_ok"))
        b1_mm, b1_ok, sub_ok, pexp_ok, gparts_ok, gT_mm, gTf_ok, gT3_ok, owner_ok = (
            sem(n) for n in ("b1_mm", "b1_ok", "sub_ok", "pexp_ok", "gparts_ok", "gT_mm", "gTf_ok", "gT3_ok", "owner_ok"))
        half_ok, ws_hi, ws_ok, h_mm, g_mm, relu_ok, hg_ok, hh_ok, hl_ok, y_mm, act_sync, pool_sync = (
            sem(n) for n in ("half_ok", "ws_hi", "ws_ok", "h_mm", "g_mm", "relu_ok", "hg_ok", "hh_ok", "hl_ok", "y_mm", "act_sync", "pool_sync"))
        y_done, yb_mm, res_ok, stored = (sem(n) for n in ("y_done", "yb_mm", "res_ok", "stored"))
        xh_ok = [sem(f"xh_ok{half}") for half in range(2)]
        xl_ok = [sem(f"xl_ok{half}") for half in range(2)]
        yT_ok = [sem(f"yT_ok{half}") for half in range(2)]

        A_CT, A_XT, A_Q, A_B1 = banks[0:2], banks[6:8], banks[0:2], banks[7]
        A_KV = [psum[:, 2:4, :], psum[:, 4:6, :]]
        S_BANK, ST_BANK, O_BANK, T_BANK, T2_BANK = banks[0:2], banks[2:5], banks[5], banks[6], banks[7]
        C_AT, C_PJ = T_BANK, T_BANK
        C_XT, C_RTT, C_RT = [banks[2], banks[3], banks[7], T_BANK], banks[1], banks[2]
        Y_BANK = banks[0:4]
        H_BANK, G_BANK = banks[4:6], banks[6:8]
        E_BANK = banks[4:8]

        ATTN_STEPS = [GROUPS - 5, GROUPS - 3, GROUPS - 1]
        PROJ_STEPS = [GROUPS - 4, GROUPS - 2, GROUPS - 1]
        RESIDUAL_STEPS = [GROUPS - 4, GROUPS - 2, GROUPS - 1]

        xf = x.rearrange("b (t p) d -> p (b t) d", p=P)
        of = out.rearrange("b (t p) d -> p (b t) d", p=P)

        def rows_to_partitions(v, n):
            return v.partition_broadcast(n)

        block = keep.enter_context(nc.Block())

        @block.sync
        def _(sp):
            for b in range(B):
                sp.dma_start(x_sb[:, TB * b:TB * b + TB, :], xf[:, TB * b:TB * b + TB, :]).then_inc(x_ld[b], 16)
            sp.dma_start(wq_sb[:, :, :], wq.rearrange("(k p) n -> p k n", p=P)).then_inc(wq_ld, 16)
            sp.dma_start(wkv_sb[:, :], wkv).then_inc(wkv_ld, 16)
            sp.dma_start(wout_sb[:, :, :], wout.rearrange("(k p) n -> p k n", p=P)).then_inc(out_w_ld, 16)
            sp.dma_start(rtw_sb[:, :, :], router_w.rearrange("(k p) n -> p k n", p=P)).then_inc(out_w_ld, 16)
            sp.dma_start(bout_sb[:, :], rows_to_partitions(bout, P)).then_inc(out_w_ld, 16)
            sp.dma_start(rtb_sb[:, :], rows_to_partitions(router_b, P)).then_inc(out_w_ld, 16)
            sp.dma_start(b2_sb[0:NE, :], rb2).then_inc(b2_ld, 16)
            sp.dma_start(b2_sb[NE:NE + NS, :], sb2).then_inc(b2_ld, 16)
            sp.wait_ge(b1_clear, 1)
            sp.dma_start(b1rows[0:RT, :], rb1.rearrange("e h -> (e h)").rearrange("(t p) -> t p", p=P)).then_inc(bias_ld, 16)
            sflat = sb1.rearrange("e h -> (e h)")
            sp.dma_start(b1rows[SB_ROW:SB_ROW + SFULL, :],
                         sflat[0:SFULL * P].rearrange("(t p) -> t p", p=P)).then_inc(bias_ld, 16)
            sp.dma_start(b1rows[SB_ROW + SFULL:TILES, 0:SREST],
                         sflat[SFULL * P:NS * HID].rearrange("(t p) -> t p", t=1)).then_inc(bias_ld, 16)

            sp.wait_ge(kd_clear, 1)
            for i in range(GROUPS):
                sp.wait_ge(t_ok, i + 1)
                if i == RING - 1:
                    sp.wait_ge(kd_clear, 2)
                if i >= RING:
                    sp.wait_ge(st_mm, 4 * (i - RING + 1))
                for j in range(GH):
                    sp.dma_start(Kd[i % RING][HR * j:HR * j + HR, j, :].bitcast(F32),
                                 QK[i % RING][HR * j:HR * j + HR, 1, :].bitcast(F32)).then_inc(kd_ld[i % RING], 16)
            sp.wait_ge(norm_ok, PAIRS)
            w1v = rw1.rearrange("e (k p) h -> p k e h", p=P)
            w1d = w1[:, :, :].rearrange("p k (e h) -> p k e h", h=HID)
            w2v = rw2.rearrange("e h n -> (e h) n").rearrange("(t p) n -> p t n", p=P)
            for c in range(2):
                e0, e1 = c * NE // 2, (c + 1) * NE // 2
                for k in range(KD):
                    sp.dma_start(w1d[:, k, e0:e1, :], w1v[:, k, e0:e1, :]).then_inc(w_ld[c], 16)
                t0, t1 = c * RT // 2, (c + 1) * RT // 2
                sp.dma_start(w2[:, t0:t1, :], w2v[:, t0:t1, :]).then_inc(w_ld[c], 16)
            for b in range(B):
                sp.wait_ge(res_ok, b + 1)
                sp.dma_start(of[:, TB * b:TB * b + TB, :], res[:, TB * b:TB * b + TB, :]).then_inc(stored, 16)
            sp.wait_ge(stored, 16 * B)

        @block.gpsimd
        def _(pool):
            steps = [0]

            def then(ins):
                steps[0] += 1
                ins.then_inc(pool_step, 1)
                pool.wait_ge(pool_step, steps[0])

            pool.memset(b1rows[:, :], 0.0).then_inc(b1_clear, 1)
            then(pool.memset(ident[:, :], 0.0))
            then(pool.affine_select(out=ident[:, :], in_=ident[:, :], compare_op=ALU.not_equal, fill=1.0,
                                    base=0, pattern=[[-1, P]], channel_multiplier=1))
            pool.tensor_copy(ident_b[:, :], ident[:, :]).then_inc(ident_ok, 1)
            pool.memset(Qx[:, :, :, R_MAX:HR].bitcast(F32), 0.0).then_inc(pads_ok, 1)
            for i in range(RING - 1):
                last = pool.memset(Kd[i][:, :, :].bitcast(F32), 0.0)
            last.then_inc(kd_clear, 1)
            Vp = Vx[:, :, :, :].rearrange("p n (m s h) r -> p (n m) s h r", s=2, h=GH)
            pool.memset(Vp[:, :, 0, :, HD:HD + 1], 1.0)
            pool.memset(Vp[:, :, 0, :, HD + 1:HR], 0.0)
            pool.memset(Vp[:, :, 1, :, 0:SLOT], 0.0)
            pool.memset(Vp[:, :, 1, :, SLOT + HD:SLOT + HD + 1], 1.0)
            pool.memset(Vp[:, :, 1, :, SLOT + HD + 1:HR], 0.0).then_inc(v_pads_ok, 1)
            for b in range(B):
                pool.wait_ge(hi_ok, 2 * b + 1)
                rows = slice(TB * b, TB * b + TB)
                q32, k32 = (qk32[b % 2][:, n].rearrange("p t (h d) -> p t h d", d=HD) for n in range(2))
                pool.tensor_tensor(Kx[:, rows, :, 2 * HD:3 * HD], k32, Kx[:, rows, :, 0:HD], ALU.subtract).then_inc(lo_ok, 1)
                pool.wait_ge(hi_ok, 2 * b + 2)
                pool.tensor_tensor(Qx[:, rows, :, HD:2 * HD], q32, Qx[:, rows, :, 0:HD], ALU.subtract).then_inc(lo_ok, 1)
            pool.wait_ge(q_mm, B)
            pool.wait_ge(kv_mm, NT)
            pool.memset(Kd[RING - 1][:, :, :].bitcast(F32), 0.0).then_inc(kd_clear, 1)

            def residual_with_bias(n):
                if n == 0:
                    pool.wait_ge(act_step, 2)
                    pool.wait_ge(out_w_ld, 64)
                    then(pool.tensor_scalar(bout_sb[:, :], bout_sb[:, :], gx[:, 0:1], None, ALU.mult))
                    pool.wait_ge(xn_ok, NT)
                pool.tensor_tensor(x_sb[:, n, :], x_sb[:, n, :], bout_sb[:, :], ALU.add).then_inc(xb_ok, 1)

            def owners():
                pool.wait_ge(rot_ok, 2 * B)
                then(pool.memset(hot[:, :], 0.0))
                for n in range(3):
                    then(pool.affine_select(out=hot[:, :], in_=hot[:, :], compare_op=ALU.not_equal, fill=1.0,
                                            base=-NE * n, pattern=[[-1, NE]], channel_multiplier=1))
                pool.tensor_copy(owner[:, :].rearrange("p (e h) -> p e h", h=HID),
                                 hot[:, :].unsqueeze(2).to_broadcast([3 * NE, NE, HID])).then_inc(owner_ok, 1)

            def shared_weights(t):
                if t == 0:
                    pool.wait_ge(ws_ld, 16 * (KD + 2))
                rows = P if t < SFULL else SREST
                src1 = w1s[:, :, P * t:P * t + rows]
                src2 = w2s[0:rows, t, :]
                pool.tensor_copy(w1h[t][:, :, 0:rows], src1).then_inc(ws_hi, 1)
                pool.tensor_copy(w2h[t][0:rows, :], src2).then_inc(ws_hi, 1)
                pool.wait_ge(ws_hi, 2 * t + 2)
                pool.tensor_tensor(w1l[t][:, :, 0:rows], src1, w1h[t][:, :, 0:rows], ALU.subtract).then_inc(ws_ok, 1)
                pool.tensor_tensor(w2l[t][0:rows, :], src2, w2h[t][0:rows, :], ALU.subtract).then_inc(ws_ok, 1)

            for n in range(NT):
                residual_with_bias(n)
            owners()
            for t in range(SHT):
                shared_weights(t)

            def shared_low_part(u):
                t, half = u // 2, u % 2
                rows = P if t < SFULL else SREST
                cols = slice(half * HALF, (half + 1) * HALF)
                pool.wait_ge(hh_ok, u + 1)
                pool.tensor_tensor(hl[t % 2][0:rows, cols], hr[half][0:rows, :], hh[t % 2][0:rows, cols],
                                   ALU.subtract).then_inc(hl_ok, 1)

            pool.wait_ge(norm_ok, PAIRS)
            pool.memset(gates[:, :, NE:NE + NS], 1.0 / NS).then_inc(half_ok, 1)
            for b in (0, 2, 3):
                cols = slice(TB * b * P, TB * (b + 1) * P)
                pool.wait_ge(xh_ok[b // (B // 2)], b % (B // 2) + 1)
                pool.tensor_tensor(xTl[:, :, cols], xT32[:, :, cols], xTh[:, :, cols], ALU.subtract).then_inc(xl_ok[b // (B // 2)], 1)
            for u in range(2 * SHT):
                shared_low_part(u)
            for c in range(2):
                pool.wait_ge(w_ld[c], 16 * (KD + 1))
                with pool.Fori(c * RT // 4, (c + 1) * RT // 4) as it:
                    for j in range(2):
                        t = it * 2 + (SHT + j)
                        k = (SHT + j) % 2
                        r = it * 2 + j
                        src1 = w1[:, :, bass.ds(r * P, P)]
                        src2 = w2[:, bass.ds(r, 1), :].rearrange("p a n -> p (a n)")
                        pool.wait_ge(h_mm, t * 2 - 2)
                        pool.nop().then_inc(pool_sync, 1)
                        pool.tensor_copy(w1h[k][:, :, :], src1).then_inc(ws_hi, 1)
                        pool.wait_ge(ws_hi, t * 2 + 1)
                        pool.nop().then_inc(pool_sync, 1)
                        pool.tensor_tensor(w1l[k][:, :, :], src1, w1h[k][:, :, :], ALU.subtract).then_inc(ws_ok, 1)
                        pool.wait_ge(y_mm, t - 1)
                        pool.nop().then_inc(pool_sync, 1)
                        pool.tensor_copy(w2h[k][:, :], src2).then_inc(ws_hi, 1)
                        pool.wait_ge(ws_hi, t * 2 + 2)
                        pool.nop().then_inc(pool_sync, 1)
                        pool.tensor_tensor(w2l[k][:, :], src2, w2h[k][:, :], ALU.subtract).then_inc(ws_ok, 1)

        @block.scalar
        def _(act):
            act.dma_start(pos_sb[:, :, :], pos.rearrange("b (t p) a -> p (b t) a", p=P)).then_inc(pos_ld, 16)
            act.dma_start(ctx_sb[:, :, :], ctx.rearrange("b (t p) c -> p (b t) c", p=P)).then_inc(ctx_ld, 16)
            act.dma_start(gx[:, :], rows_to_partitions(g_xattn, P)).then_inc(gate_ld, 16)
            act.dma_start(gf[:, :], rows_to_partitions(g_ffn, P)).then_inc(gate_ld, 16)
            act.wait_ge(ang_ok, 1)
            act.activation(trig[:, :, :, :], ang[:, :, :].rearrange("p s (t f) -> p s t f", f=4), ACT.Sin).then_inc(trig_ok, 1)

            def square_root(n, tiles):
                act.wait_ge(veps_ok, n)
                act.activation(root[:, tiles], veps[:, tiles], ACT.Sqrt).then_inc(root_ok, 1)

            def evacuate(b):
                act.wait_ge(xT_mm, b + 1)
                act.activation(xnT[:, b], A_XT[b % 2].rearrange("p (t k q) -> p t k q", t=TB, k=KD), ACT.Copy).then_inc(xT_ok, 1)

            for c in range(2):
                act.wait_ge(cT_mm, c + 1)
                act.activation(ctxT[:, c * NT // 2:(c + 1) * NT // 2, :], A_CT[c].rearrange("p (t q) -> p t q", q=P),
                               ACT.Copy).then_inc(cT_ok, 1)
            square_root(1, slice(0, NT))

            def read_values(b):
                act.wait_ge(kv_mm, TB * (b + 1))
                for second in range(2):
                    act.activation(Vpairs[:, TB * b:TB * b + TB, :, second, :, SLOT * second:SLOT * second + HD],
                                   A_KV[b % 2][:, :, D:2 * D].rearrange("p t (m s h d) -> p t m s h d", s=2, h=GH, d=HD)[:, :, :, second],
                                   ACT.Copy).then_inc(v_ok, 1)

            def evacuate_t(i):
                act.wait_ge(t_mm, i + 1)
                if i >= RING:
                    act.wait_ge(s_mm, 4 * (i - RING + 1))
                    act.wait_ge(kd_ld[i % RING], 64 * (i // RING))
                act.activation(QK[i % RING][:, :, :], T_BANK[:, :].rearrange("p (a n) -> p a n", a=2), ACT.Copy).then_inc(t_ok, 1)

            def high_parts(b):
                rows = slice(TB * b, TB * b + TB)
                q32, k32 = (qk32[b % 2][:, n].rearrange("p t (h d) -> p t h d", d=HD) for n in range(2))
                act.wait_ge(rot_ok, 2 * b + 1)
                act.activation(Kx[:, rows, :, 0:HD], k32, ACT.Copy).then_inc(hi_ok, 1)
                act.activation(Kx[:, rows, :, HD:2 * HD], k32, ACT.Copy)
                act.wait_ge(rot_ok, 2 * b + 2)
                act.activation(Qx[:, rows, :, 0:HD], q32, ACT.Copy).then_inc(hi_ok, 1)
                act.activation(Qx[:, rows, :, 2 * HD:3 * HD], q32, ACT.Copy).then_inc(qkv_read, 1)

            read_values(0)
            read_values(1)
            evacuate(0)
            evacuate(1)
            for k in range(KD):
                act.dma_start(w1s[:, k, :].rearrange("p (e h) -> p e h", h=HID),
                              sw1.rearrange("e (k p) h -> p k e h", p=P)[:, k]).then_inc(ws_ld, 16)
            sflat2 = sw2.rearrange("e h n -> (e h) n")
            act.dma_start(w2s[:, 0:SFULL, :], sflat2[0:SFULL * P, :].rearrange("(t p) n -> p t n", p=P)).then_inc(ws_ld, 16)
            act.dma_start(w2s[0:SREST, SFULL, :], sflat2[SFULL * P:NS * HID, :]).then_inc(ws_ld, 16)
            for b in range(B):
                high_parts(b)
                if b + 2 < B:
                    read_values(b + 2)
                    evacuate(b + 2)
                if b == B - 3:
                    evacuate_t(0)
                if b == B - 2:
                    evacuate_t(1)
                    evacuate_t(2)
                    act.wait_ge(gate_ld, 32)
                    act.activation(gx[:, :], gx[:, :], ACT.Tanh).then_inc(act_step, 1)
                    act.activation(gf[:, :], gf[:, :], ACT.Tanh).then_inc(act_step, 1)

            def exponentials(g, n):
                kt, hp = n // 2, n % 2
                if n == 0 and g >= 2:
                    act.wait_ge(pv_mm, 2 * (g - 1))
                act.wait_ge(st_mm, 4 * g + n + 1)
                act.activation(probs[g % 2][:, kt, 2 * hp:2 * hp + 2, :],
                               ST_BANK[(4 * g + n) % 3][:, :].rearrange("p (h q) -> p h q", h=2),
                               ACT.Exp, scale=SCALE).then_inc(exp_ok, 1)

            def step(i):
                g = i - 1
                if 0 <= g < GROUPS:
                    act.wait_ge(t2_mm, g + 1)
                    if g >= 2:
                        act.wait_ge(st_mm, 4 * (g - 1))
                    act.activation(QT[g % 2][:, :], T2_BANK[:, 0:N], ACT.Copy).then_inc(q2_ok, 1)
                if i + AHEAD < GROUPS:
                    evacuate_t(i + AHEAD)
                if 0 <= g < GROUPS:
                    exponentials(g, 0)
                    exponentials(g, 1)
                p = (i - 3) // 2
                if i % 2 and 0 <= p < PAIRS:
                    act.wait_ge(pv_mm, 2 * (i - 1))
                    if p >= 2:
                        act.wait_ge(ot_mm, p - 1)
                    act.activation(oT[p % 2][:, :], O_BANK[:, 0:N], ACT.Copy).then_inc(o_ok, 1)
                if i in ATTN_STEPS[1:]:
                    transposed_attention(ATTN_STEPS.index(i))
                if 0 <= g < GROUPS:
                    exponentials(g, 2)
                    exponentials(g, 3)
                if i == ATTN_STEPS[0]:
                    transposed_attention(0)

            def transposed_attention(b):
                act.wait_ge(aT_mm, b + 1)
                if b >= 2:
                    act.wait_ge(pj_mm, b - 1)
                act.activation(attnT[:, b % 2], C_AT.rearrange("p (t k q) -> p t k q", t=TB, k=KD), ACT.Copy).then_inc(aT_ok, 1)

            for i in range(GROUPS + 3):
                step(i)

            square_root(2, slice(0, NT - TB))
            act.wait_ge(norm_ok, PAIRS)
            transposed_attention(B - 1)

            act.wait_ge(b1_ok, 2)

            def shared_hidden(u):
                t, half = u // 2, u % 2
                rows = P if t < SFULL else SREST
                act.wait_ge(h_mm, u + 1)
                if u >= 2:
                    act.wait_ge(hl_ok, u - 1)
                act.activation(hr[half][0:rows, :], H_BANK[half][0:rows, :], ACT.Relu,
                               bias=b1half[0:rows, t:t + 1], scale=1.0 / NS).then_inc(relu_ok, 1)
                if t >= 2:
                    act.wait_ge(y_mm, t - 1)
                act.wait_ge(relu_ok, u + 1)
                act.activation(hh[t % 2][0:rows, half * HALF:(half + 1) * HALF], hr[half][0:rows, :],
                               ACT.Copy).then_inc(hh_ok, 1)

            def second_rows(b):
                act.wait_ge(x2T_mm, b + 1)
                cols = slice(TB * b * P, TB * (b + 1) * P)
                act.activation(xT32[:, :, cols].rearrange("p k (t q) -> p k t q", t=TB),
                               C_XT[b].rearrange("p (t k q) -> p k t q", t=TB, k=KD), ACT.Copy).then_inc(x2T_ok, 1)

            def second_rows_high(b):
                cols = slice(TB * b * P, TB * (b + 1) * P)
                act.wait_ge(x2T_ok, b + 1)
                act.activation(xTh[:, :, cols], xT32[:, :, cols], ACT.Copy).then_inc(xh_ok[b // (B // 2)], 1)

            for b in range(B - 1):
                second_rows(b)
            square_root(3, slice(NT - TB, NT))
            second_rows_high(0)
            second_rows_high(1)
            second_rows_high(2)
            second_rows(B - 1)
            second_rows_high(B - 1)
            act.wait_ge(lgT_mm, B)
            act.activation(lgT[:, :], C_RTT[:, 0:N], ACT.Copy).then_inc(lgT_ok, 1)
            shared_hidden(0)
            act.wait_ge(sub_ok, 1)
            act.activation(pr[:, :, :], lg[:, :, :], ACT.Exp).then_inc(pexp_ok, 1)

            for u in range(1, 2 * SHT):
                shared_hidden(u)
            for n, half in enumerate((1, 0)):
                act.wait_ge(gT_mm, n + 2)
                act.activation(gTf[:, half * HALF:(half + 1) * HALF], G_BANK[half][0:NE + NS, :],
                               ACT.Copy).then_inc(gTf_ok, 1)
            with act.Fori(0, RT // 2) as it:
                for j in range(2):
                    for half in range(2):
                        u = it * 4 + (2 * (SHT + j) + half)
                        act.wait_ge(h_mm, u + 1)
                        act.wait_ge(hl_ok, u - 1)
                        act.nop().then_inc(act_sync, 1)
                        act.activation(hr[half][:, :], H_BANK[half][:, :], ACT.Relu,
                                       bias=b1cols[:, bass.ds(it * 2 + j, 1)]).then_inc(relu_ok, 1)
            for half in range(2):
                act.wait_ge(y_done, half + 1)
                act.activation(yT[:, 0, half * HALF:(half + 1) * HALF], Y_BANK[half][:, :], ACT.Copy).then_inc(yT_ok[half], 1)

        @block.vector
        def _(dve):
            steps = [0]

            def then(ins):
                steps[0] += 1
                ins.then_inc(dve_step, 1)
                dve.wait_ge(dve_step, steps[0])

            TWO_PI = 2 * np.pi
            C1 = float(np.float32(6.28125))
            C2 = float(np.float32(TWO_PI - 6.28125))
            ROUND = float(1.5 * 2 ** 23)
            PI_BELOW = float(np.nextafter(np.float32(np.pi), np.float32(0)))
            FREQ1 = float(np.float32(10000.0) ** np.float32(-0.5))

            dve.memset(Kx[:, :, :, R_MAX:R_MAX + 2].bitcast(F32), 1.0)
            dve.memset(Kx[:, :, :, R_MAX + 2:HR].bitcast(F32), 0.0).then_inc(pads_ok, 1)
            dve.wait_ge(pos_ld, 16)
            sine = ang[:, 0].rearrange("p (t a f) -> p t a f", a=2, f=2)
            dve.tensor_scalar(sine[:, :, :, 0], pos_sb[:, :, :], 1.0, None, ALU.mult)
            then(dve.tensor_scalar(sine[:, :, :, 1], pos_sb[:, :, :], FREQ1, None, ALU.mult))
            then(dve.tensor_scalar(ang[:, 1], ang[:, 0], float(np.pi / 2), None, ALU.add))
            then(dve.tensor_scalar(turns[:, :, :], ang[:, :, :], float(1 / TWO_PI), ROUND, ALU.mult, ALU.add))
            then(dve.tensor_scalar(turns[:, :, :], turns[:, :, :], ROUND, None, ALU.subtract))
            then(dve.scalar_tensor_tensor(out=ang[:, :, :], in0=turns[:, :, :], scalar=-C1, in1=ang[:, :, :],
                                          op0=ALU.mult, op1=ALU.add))
            then(dve.scalar_tensor_tensor(out=ang[:, :, :], in0=turns[:, :, :], scalar=-C2, in1=ang[:, :, :],
                                          op0=ALU.mult, op1=ALU.add))
            dve.tensor_scalar(ang[:, :, :], ang[:, :, :], PI_BELOW, -PI_BELOW, ALU.min, ALU.max).then_inc(ang_ok, 1)

            def statistics(first, n):
                for t in range(first, first + n):
                    ins = dve.bn_stats(stats[:, t, :], x_sb[:, t, :])
                return ins

            roots = [0]

            def variances(first, n):
                rows = slice(first, first + n)
                for t in range(first, first + n):
                    ins = dve.bn_aggr(mv[:, t, :], stats[:, t, :])
                then(ins)
                dve.tensor_scalar(veps[:, rows], mv[:, rows, 1], EPS, None, ALU.add).then_inc(veps_ok, 1)

            def inverse_deviations(first, n):
                rows = slice(first, first + n)
                roots[0] += 1
                dve.wait_ge(root_ok, roots[0])
                then(dve.reciprocal(rstd[:, rows], root[:, rows]))
                then(dve.tensor_tensor(newton[:, rows], rstd[:, rows], rstd[:, rows], ALU.mult))
                then(dve.tensor_tensor(newton[:, rows], newton[:, rows], veps[:, rows], ALU.mult))
                then(dve.tensor_scalar(newton[:, rows], newton[:, rows], -0.5, 1.5, ALU.mult, ALU.add))
                then(dve.tensor_tensor(rstd[:, rows], rstd[:, rows], newton[:, rows], ALU.mult))

            def normalise_rows(b, dst, done):
                for t in range(TB):
                    n = TB * b + t
                    dve.tensor_scalar(dst[:, t, :], x_sb[:, n, :], mv[:, n, 0:1], rstd[:, n:n + 1],
                                      ALU.subtract, ALU.mult).then_inc(done, 1)

            def multiply_turns(b, n, psum):
                rows = slice(TB * b, TB * b + TB)
                c8, s8 = (v[:, rows].rearrange("p t f c -> p t (f c)").unsqueeze(2).to_broadcast([P, TB, H, 8])
                          for v in (cos8, sin8))
                src = psum.rearrange("p t (h d) -> p t h d", d=HD)
                if b >= 2:
                    dve.wait_ge(rot_ok, 2 * (b - 1))
                for part, factor in enumerate((c8, s8)):
                    ins = dve.tensor_tensor(turned[b % 2][:, n, part].rearrange("p t (h d) -> p t h d", d=HD),
                                            src, factor, ALU.mult)
                ins.then_inc(turn_mul, 1)

            def add_turns(b, n):
                pairs = [v.rearrange("p t (m c) -> p (t m) c", c=2)
                         for v in (turned[b % 2][:, n, 0], turned[b % 2][:, n, 1], qk32[b % 2][:, n])]
                dve.wait_ge(turn_mul, 2 * b + 2 - n)
                if b >= 2:
                    dve.wait_ge(qkv_read, b - 1)
                    dve.wait_ge(lo_ok, 2 * (b - 1))
                dve.tensor_tensor(pairs[2][:, :, 0], pairs[0][:, :, 0], pairs[1][:, :, 1], ALU.add)
                dve.tensor_tensor(pairs[2][:, :, 1], pairs[0][:, :, 1], pairs[1][:, :, 0], ALU.add).then_inc(rot_ok, 1)

            for b in range(B):
                dve.wait_ge(x_ld[b], 16)
                ins = statistics(TB * b, TB)
            then(ins)
            variances(0, NT)
            inverse_deviations(0, NT)
            for b in range(B):
                normalise_rows(b, xn[:, b], xn_ok)
            dve.wait_ge(trig_ok, 1)
            dve.tensor_copy(cos8[:, :, :, :], trig[:, 1].unsqueeze(3).to_broadcast([P, NT, 4, 2]))
            dve.tensor_copy(sin8[:, :, :, 0], trig[:, 0])
            then(dve.tensor_scalar(sin8[:, :, :, 1], trig[:, 0], -1.0, None, ALU.mult))
            for b in range(B):
                dve.wait_ge(v_ok, TB * (b + 1))
                multiply_turns(b, 1, A_KV[b % 2][:, :, 0:D])
                dve.wait_ge(q_mm, b + 1)
                multiply_turns(b, 0, A_Q[b % 2].rearrange("p (t n) -> p t n", t=TB))
                if b == B - 1:
                    dve.wait_ge(b1_mm, 1)
                    dve.tensor_copy(b1cols[:, :], A_B1[:, 0:TILES]).then_inc(b1_ok, 1)
                    dve.tensor_scalar(b1half[:, :], A_B1[:, SB_ROW:TILES], 1.0 / NS, None, ALU.mult).then_inc(b1_ok, 1)
                add_turns(b, 1)
                add_turns(b, 0)

            def row_max(i, n):
                qt, hp = n // 2, n % 2
                if n == 0 and i >= 2:
                    dve.wait_ge(m_ok, i - 1)
                dve.wait_ge(s_mm, 4 * i + n + 1)
                dve.tensor_reduce(nmax[i % 2][:, qt, 2 * hp:2 * hp + 2],
                                  S_BANK[n % 2][:, :].rearrange("p (h k) -> p h k", h=2),
                                  AX.X, ALU.max, negate=True).then_inc(s_max, 1)

            def normalise(p):
                b, g = p // (NG // 2), p % (NG // 2)
                o = T2_BANK[:, 0:TB * P].rearrange("p (t h s c) -> p t s h c", t=TB, s=2, c=SLOT)
                if p >= 2:
                    dve.wait_ge(norm_ok, p - 1)
                dve.wait_ge(ot_mm, p + 1)
                dve.reciprocal(rden[p % 2][:, :, :, :], o[:, :, :, :, HD]).then_inc(rd_ok, 1)
                dve.wait_ge(rd_ok, p + 1)
                for second in range(2):
                    first = GH * HD * (2 * g + second)
                    dst = attn[:, TB * b:TB * b + TB, first:first + GH * HD].rearrange("p t (h d) -> p t h d", d=HD)
                    ins = dve.tensor_tensor(dst, o[:, :, second, :, 0:HD],
                                            rden[p % 2][:, :, second].unsqueeze(3).to_broadcast([P, TB, GH, HD]), ALU.mult)
                ins.then_inc(norm_ok, 1)

            def maxima(g):
                b, n = g // NG, g % NG
                dst = Qx[:, TB * b:TB * b + TB, GH * n:GH * n + GH, :]
                dve.wait_ge(s_max, 4 * g + 4)
                dve.tensor_copy(dst[:, :, :, R_MAX], nmax[g % 2][:, :, :]).then_inc(mhi_ok, 1)
                dve.wait_ge(mhi_ok, g + 1)
                dve.tensor_tensor(dst[:, :, :, R_MAX + 1], nmax[g % 2][:, :, :], dst[:, :, :, R_MAX],
                                  ALU.subtract).then_inc(m_ok, 1)

            def residual(b):
                rows = slice(TB * b, TB * b + TB)
                if b == 0:
                    dve.wait_ge(act_step, 2)
                    dve.wait_ge(xb_ok, NT)
                dve.wait_ge(pj_mm, b + 1)
                dve.scalar_tensor_tensor(out=x_sb[:, rows, :], in0=C_PJ.rearrange("p (t n) -> p t n", t=TB),
                                         scalar=gx[:, 0:1], in1=x_sb[:, rows, :],
                                         op0=ALU.mult, op1=ALU.add).then_inc(pj_ok, 1)
                dve.wait_ge(pj_ok, b + 1)
                then(statistics(TB * b, TB))

            for i in range(GROUPS + 3):
                if i < GROUPS:
                    row_max(i, 0)
                    row_max(i, 1)
                    row_max(i, 2)
                if i >= 4 and i % 2 == 0:
                    normalise((i - 4) // 2)
                if i < GROUPS:
                    row_max(i, 3)
                    maxima(i)
                if i in RESIDUAL_STEPS:
                    residual(RESIDUAL_STEPS.index(i))
                if i == RESIDUAL_STEPS[-1]:
                    variances(0, NT - TB)

            inverse_deviations(0, NT - TB)
            for b in range(B - 1):
                normalise_rows(b, xn2[:, b], xn2_ok)
            residual(B - 1)
            variances(NT - TB, TB)
            inverse_deviations(NT - TB, TB)
            normalise_rows(B - 1, xn2[:, B - 1], xn2_ok)
            cols = slice(TB * P, 2 * TB * P)
            dve.wait_ge(xh_ok[0], 2)
            dve.tensor_tensor(xTl[:, :, cols], xT32[:, :, cols], xTh[:, :, cols], ALU.subtract).then_inc(xl_ok[0], 1)
            dve.wait_ge(rt_mm, 1)
            for t in range(TB):
                dve.tensor_tensor(lg[:, :, :].rearrange("p (b t) e -> p b t e", t=TB)[:, :, t],
                                  C_RT[:, t * P:(t + 1) * P].rearrange("p (b e) -> p b e", b=B),
                                  rtb_sb[:, :].unsqueeze(1).to_broadcast([P, B, NE]), ALU.add).then_inc(lg_ok, 1)

            def per_expert(v):
                return v.unsqueeze(2).to_broadcast([P, NT, NE])

            dve.wait_ge(lg_ok, TB)
            then(dve.tensor_reduce(red[:, 0], lg[:, :, :], AX.X, ALU.max))
            dve.tensor_tensor(lg[:, :, :], lg[:, :, :], per_expert(red[:, 0]), ALU.subtract).then_inc(sub_ok, 1)
            for c in cum:
                dve.memset(c[:, :, 0:PAD], 0.0)
            dve.wait_ge(pexp_ok, 1)
            then(dve.tensor_reduce(red[:, 1], pr[:, :, :], AX.X, ALU.add))
            then(dve.reciprocal(red[:, 2], red[:, 1]))
            then(dve.tensor_tensor(pr[:, :, :], pr[:, :, :], per_expert(red[:, 2]), ALU.mult))
            for t in range(NT):
                ins = dve.max(top8[:, t, :], pr[:, t, :])
            then(ins)
            sixth = per_expert(top8[:, :, TOPK - 1])
            then(dve.tensor_tensor(gt[:, :, :], pr[:, :, :], sixth, ALU.is_gt))
            dve.tensor_reduce(red[:, 3], gt[:, :, :], AX.X, ALU.add)
            dve.tensor_tensor(eq[:, :, :], pr[:, :, :], sixth, ALU.is_equal)
            then(dve.tensor_tensor(cum[0][:, :, PAD:], pr[:, :, :], sixth, ALU.is_equal))
            then(dve.tensor_scalar(red[:, 0], red[:, 3], -1.0, float(TOPK), ALU.mult, ALU.add))
            shift, a = 1, 0
            while shift < NE:
                then(dve.tensor_tensor(cum[1 - a][:, :, PAD:], cum[a][:, :, PAD:],
                                       cum[a][:, :, PAD - shift:PAD + NE - shift], ALU.add))
                shift, a = 2 * shift, 1 - a
            then(dve.tensor_tensor(sel[:, :, :], cum[a][:, :, PAD:], per_expert(red[:, 0]), ALU.is_le))
            then(dve.tensor_tensor(eq[:, :, :], eq[:, :, :], sel[:, :, :], ALU.mult))
            then(dve.tensor_tensor(gt[:, :, :], gt[:, :, :], eq[:, :, :], ALU.add))
            then(dve.tensor_tensor(sel[:, :, :], gt[:, :, :], pr[:, :, :], ALU.mult))
            then(dve.tensor_reduce(red[:, 1], sel[:, :, :], AX.X, ALU.add))
            then(dve.reciprocal(red[:, 2], red[:, 1]))
            dve.wait_ge(half_ok, 1)
            then(dve.tensor_tensor(gates[:, :, 0:NE], sel[:, :, :], per_expert(red[:, 2]), ALU.mult))
            then(dve.tensor_copy(gparts[:, :, 0, :], gates[:, :, 0:NE]))
            then(dve.tensor_tensor(sel[:, :, :], gates[:, :, 0:NE], gparts[:, :, 0, :], ALU.subtract))
            then(dve.tensor_copy(gparts[:, :, 1, :], sel[:, :, :]))
            then(dve.tensor_tensor(sel[:, :, :], sel[:, :, :], gparts[:, :, 1, :], ALU.subtract))
            dve.tensor_copy(gparts[:, :, 2, :], sel[:, :, :]).then_inc(gparts_ok, 1)

            dve.wait_ge(gT_mm, 1)
            dve.tensor_copy(gT3[:, :], G_BANK[0].bitcast(BF16)[0:3 * NE, :]).then_inc(gT3_ok, 1)
            with dve.Fori(0, RT // 2) as it:
                for j in range(2):
                    for half in range(2):
                        tt = SHT + j
                        u = it * 4 + (2 * tt + half)
                        r = it * 4 + (2 * j + half)
                        cols = slice(half * HALF, (half + 1) * HALF)
                        dve.wait_ge(hl_ok, u - 1)
                        dve.wait_ge(g_mm, r + 1)
                        dve.wait_ge(relu_ok, u + 1)
                        dve.tensor_tensor(hg[half][:, :], hr[half][:, :], G_BANK[half][:, :], ALU.mult).then_inc(hg_ok, 1)
                        dve.wait_ge(y_mm, it * 2 + (tt - 1))
                        dve.wait_ge(hg_ok, r + 1)
                        dve.tensor_copy(hh[tt % 2][:, cols], hg[half][:, :]).then_inc(hh_ok, 1)
                        dve.wait_ge(hh_ok, u + 1)
                        dve.tensor_tensor(hl[tt % 2][:, cols], hg[half][:, :], hh[tt % 2][:, cols],
                                          ALU.subtract).then_inc(hl_ok, 1)
            def second_half_rows(half):
                dve.wait_ge(y_done, half + 1)
                dve.tensor_copy(yT[:, 1, half * HALF:(half + 1) * HALF], Y_BANK[2 + half][:, :]).then_inc(yT_ok[half], 1)

            second_half_rows(0)
            second_half_rows(1)
            for b in range(B):
                rows = slice(TB * b, TB * b + TB)
                dve.wait_ge(yb_mm, b + 1)
                dve.scalar_tensor_tensor(out=res[:, rows, :], in0=E_BANK[b].rearrange("p (t n) -> p t n", t=TB),
                                         scalar=gf[:, 0:1], in1=x_sb[:, rows, :],
                                         op0=ALU.mult, op1=ALU.add).then_inc(res_ok, 1)

        @block.tensor
        def _(pe):
            pe.wait_ge(ident_ok, 1)
            warmed = [0]

            def keep_warm(n, bank):
                for _ in range(n):
                    ins = pe.matmul(bank[:, 0:P], ident[:, :], ident[:, :], start=True, stop=True)
                ins.then_inc(warm, 1)
                warmed[0] += 1
                pe.wait_ge(warm, warmed[0])

            keep_warm(WARM_UP, A_B1)
            pe.wait_ge(ctx_ld, 16)
            for c in range(2):
                for t in range(NT // 2):
                    ins = pe.transpose(A_CT[c][:, t * P:(t + 1) * P], ctx_sb[:, c * NT // 2 + t, :], ident[:, :])
                ins.then_inc(cT_mm, 1)

            def transposed_rows(b):
                pe.wait_ge(xn_ok, TB * (b + 1))
                if b >= 2:
                    pe.wait_ge(xT_ok, b - 1)
                for t in range(TB):
                    for k in range(KD):
                        n = (t * KD + k) * P
                        ins = pe.transpose(A_XT[b % 2][:, n:n + P], xn[:, b, t, k * P:(k + 1) * P], ident[:, :])
                ins.then_inc(xT_mm, 1)

            def keys_values(b):
                pe.wait_ge(wkv_ld, 16)
                if b >= 2:
                    pe.wait_ge(turn_mul, 2 * (b - 2) + 1)
                    pe.wait_ge(v_ok, TB * (b - 1))
                for t in range(TB):
                    pe.matmul(A_KV[b % 2][:, t, :], ctxT[:, TB * b + t, :], wkv_sb[:, :], start=True, stop=True).then_inc(kv_mm, 1)

            def queries(b):
                pe.wait_ge(xT_ok, b + 1)
                pe.wait_ge(wq_ld, 16)
                if b >= 2:
                    pe.wait_ge(turn_mul, 2 * (b - 1))
                for t in range(TB):
                    for k in range(KD):
                        ins = pe.matmul(A_Q[b % 2][:, t * D:(t + 1) * D], xnT[:, b, t, k, :], wq_sb[:, k, :],
                                        start=(k == 0), stop=(k == KD - 1))
                ins.then_inc(q_mm, 1)

            pe.wait_ge(cT_ok, 2)
            keys_values(0)
            keys_values(1)
            transposed_rows(0)
            transposed_rows(1)
            queries(0)
            queries(1)
            keys_values(2)
            transposed_rows(2)
            queries(2)
            keys_values(3)
            transposed_rows(3)

            def transposes(i):
                b, g = i // NG, i % NG
                if g == 0:
                    pe.wait_ge(qkv_read, b + 1)
                    pe.wait_ge(lo_ok, 2 * (b + 1))
                if i:
                    pe.wait_ge(t_ok, i)
                for b_done, step in enumerate(ATTN_STEPS):
                    if i - AHEAD == step + 1:
                        pe.wait_ge(aT_ok, b_done + 1)
                for b_done, step in enumerate(PROJ_STEPS):
                    if i - AHEAD == step + 1:
                        pe.wait_ge(pj_ok, b_done + 1)
                for a, src in enumerate((Qx, Kx)):
                    for t in range(TB):
                        n = (a * TB + t) * P
                        ins = pe.transpose(T_BANK[:, n:n + P],
                                           src[:, TB * b + t, GH * g:GH * g + GH, :].rearrange("p h r -> p (h r)").bitcast(F32),
                                           ident[:, :])
                ins.then_inc(t_mm, 1)

            def scores(i, n):
                qt, hp = n // 2, n % 2
                if n == 0:
                    pe.wait_ge(kd_ld[i % RING], 64 * (i // RING + 1))
                    pe.wait_ge(t_ok, i + 1)
                if 4 * i + n >= 2:
                    pe.wait_ge(s_max, 4 * i + n - 1)
                pe.matmul(S_BANK[n % 2], QK[i % RING][:, 0, qt * P:(qt + 1) * P], Kd[i % RING][:, 2 * hp:2 * hp + 2, :],
                          start=True, stop=True).then_inc(s_mm, 1)

            def transposed_with_max(i):
                b, g = i // NG, i % NG
                pe.wait_ge(m_ok, i + 1)
                if i >= 1:
                    pe.wait_ge(q2_ok, i)
                if i >= 4:
                    pe.wait_ge(norm_ok, (i - 2) // 2)
                for t in range(TB):
                    ins = pe.transpose(T2_BANK[:, t * P:(t + 1) * P],
                                       Qx[:, TB * b + t, GH * g:GH * g + GH, :].rearrange("p h r -> p (h r)").bitcast(F32),
                                       ident[:, :])
                ins.then_inc(t2_mm, 1)

            def shifted_scores(i, n):
                kt, hp = n // 2, n % 2
                if n == 0:
                    pe.wait_ge(q2_ok, i + 1)
                if 4 * i + n >= 3:
                    pe.wait_ge(exp_ok, 4 * i + n - 2)
                for h in range(2):
                    ins = pe.matmul(ST_BANK[(4 * i + n) % 3][:, h * N:(h + 1) * N],
                                    Kd[i % RING][:, 2 * hp + h, kt * P:(kt + 1) * P], QT[i % 2][:, :], start=True, stop=True)
                ins.then_inc(st_mm, 1)

            def values(i, kt):
                b, g = i // NG, i % NG
                pe.wait_ge(exp_ok, 4 * i + 2 * (kt + 1))
                second = i % 2
                if kt == 0 and not second and i:
                    pe.wait_ge(o_ok, i // 2)
                for h in range(GH):
                    ins = pe.matmul(O_BANK[HR * h:HR * h + HR, 0:N], Vx[:, TB * b + kt, GH * g + h, :], probs[i % 2][:, kt, h, :],
                                    start=(kt == 0 and not second), stop=(kt == TB - 1 and bool(second)),
                                    skip_group_check=True)
                ins.then_inc(pv_mm, 1)

            def outputs(p):
                pe.wait_ge(o_ok, p + 1)
                pe.wait_ge(q2_ok, min(2 * p + 4, GROUPS))
                if p:
                    pe.wait_ge(norm_ok, p)
                for t in range(TB):
                    ins = pe.transpose(T2_BANK[:, t * P:(t + 1) * P], oT[p % 2][:, t * P:(t + 1) * P], ident[:, :])
                ins.then_inc(ot_mm, 1)

            pe.wait_ge(pads_ok, 2)
            pe.wait_ge(xT_ok, 3)
            transposes(0)
            queries(3)
            pe.wait_ge(bias_ld, 48)
            pe.wait_ge(xT_ok, 4)
            pe.transpose(A_B1[:, 0:TILES], b1rows[:, :], ident[0:TILES, 0:TILES]).then_inc(b1_mm, 1)
            transposes(1)
            transposes(2)
            pe.wait_ge(turn_mul, 2 * (B - 1))
            pe.wait_ge(v_ok, TB * (B - 1))
            keep_warm(WARM_START, A_KV[0][:, 0])
            pe.wait_ge(v_pads_ok, 1)
            pe.wait_ge(turn_mul, 2 * B)
            pe.wait_ge(v_ok, NT)
            pe.wait_ge(b1_ok, 2)

            def attention_transposed(b):
                pe.wait_ge(norm_ok, NG // 2 * (b + 1))
                pe.wait_ge(t_ok, min(ATTN_STEPS[b] + AHEAD + 1, GROUPS) if b < B - 1 else GROUPS)
                if b:
                    pe.wait_ge(pj_ok, b)
                for t in range(TB):
                    for k in range(KD):
                        n = (t * KD + k) * P
                        ins = pe.transpose(C_AT[:, n:n + P], attn[:, TB * b + t, k * P:(k + 1) * P], ident[:, :])
                ins.then_inc(aT_mm, 1)

            def output_projection(b):
                pe.wait_ge(out_w_ld, 64)
                pe.wait_ge(aT_ok, b + 1)
                if b < B - 1:
                    pe.wait_ge(t_ok, min(PROJ_STEPS[b] + AHEAD + 1, GROUPS))
                for t in range(TB):
                    for k in range(KD):
                        ins = pe.matmul(C_PJ[:, t * D:(t + 1) * D], attnT[:, b % 2, t, k, :], wout_sb[:, k, :],
                                        start=(k == 0), stop=(k == KD - 1))
                ins.then_inc(pj_mm, 1)

            for i in range(GROUPS + 3):
                new, shifted, weighted = i < GROUPS, 0 <= i - 1 < GROUPS, 0 <= i - 2 < GROUPS
                if i == 0:
                    scores(i, 0)
                    scores(i, 1)
                if weighted:
                    values(i - 2, 0)
                if shifted:
                    transposed_with_max(i - 1)
                if i + AHEAD < GROUPS:
                    transposes(i + AHEAD)
                elif i == ATTN_STEPS[1]:
                    attention_transposed(1)
                elif i == PROJ_STEPS[1]:
                    output_projection(1)
                elif i == ATTN_STEPS[2]:
                    attention_transposed(2)
                if new:
                    scores(i, 2)
                if i >= 4 and i % 2 == 0:
                    outputs((i - 4) // 2)
                if shifted:
                    shifted_scores(i - 1, 0)
                    shifted_scores(i - 1, 1)
                if new:
                    scores(i, 3)
                if weighted:
                    values(i - 2, 1)
                if shifted:
                    shifted_scores(i - 1, 2)
                    shifted_scores(i - 1, 3)
                if i + 1 < GROUPS:
                    scores(i + 1, 0)
                    scores(i + 1, 1)
                if i > GROUPS:
                    keep_warm(3, S_BANK[0])
                if i == ATTN_STEPS[0]:
                    attention_transposed(0)
                if i in (PROJ_STEPS[0], PROJ_STEPS[2]):
                    output_projection(PROJ_STEPS.index(i))

            keep_warm(3, S_BANK[0])
            attention_transposed(B - 1)
            keep_warm(4, S_BANK[0])
            output_projection(B - 1)

            def second_rows_transposed(b):
                pe.wait_ge(xn2_ok, TB * (b + 1))
                for t in range(TB):
                    for k in range(KD):
                        n = (t * KD + k) * P
                        ins = pe.transpose(C_XT[b][:, n:n + P], xn2[:, b, t, k * P:(k + 1) * P], ident[:, :])
                ins.then_inc(x2T_mm, 1)

            def router_scores(b):
                pe.wait_ge(x2T_ok, b + 1)
                for k in range(KD):
                    ins = pe.matmul(C_RTT[NE * b:NE * b + NE, 0:N], rtw_sb[:, k, :],
                                    xT32[:, k, N * b:N * b + N], start=(k == 0), stop=(k == KD - 1))
                ins.then_inc(lgT_mm, 1)

            def hidden(t, k2, rows, halves=(0, 1), r=None):
                for half in halves:
                    u = t * 2 + half
                    static = isinstance(t, int)
                    if not static or t:
                        pe.wait_ge(relu_ok, u - 1)
                    if not static or t > SHT:
                        pe.wait_ge(hl_ok, u - 1)
                    pe.wait_ge(ws_ok, t * 2 + 1)
                    cols = slice(half * HALF, (half + 1) * HALF)
                    parts = [(w, v, k) for w, v in ((w1h, xTh), (w1l, xTh), (w1h, xTl)) for k in range(KD)]
                    for n, (w, v, k) in enumerate(parts):
                        if isinstance(t, int) and t == 0 and n in (0, 2 * KD):
                            pe.wait_ge((xl_ok if n else xh_ok)[half], B // 2)
                        ins = pe.matmul(H_BANK[half][0:rows, :], w[k2][:, k, 0:rows], v[:, k, cols],
                                        start=(n == 0), stop=(n == len(parts) - 1))
                    ins.then_inc(h_mm, 1)
                    if r is not None:
                        if isinstance(r, int) and r == 0 and half == 0:
                            pe.wait_ge(gTf_ok, 2)
                        pe.matmul(G_BANK[half], owner[:, bass.ds(r * P, P)], gT3[:, cols],
                                  start=True, stop=True).then_inc(g_mm, 1)

            def result(t, k2, rows, halves=(0, 1), first=False, last=False):
                pe.wait_ge(ws_ok, t * 2 + 2)
                for half in halves:
                    pe.wait_ge(hl_ok, t * 2 + half + 1)
                    cols = slice(half * HALF, (half + 1) * HALF)
                    for k in range(KD):
                        wc = slice(k * P, (k + 1) * P)
                        for n, (w, v) in enumerate(((w2h, hh), (w2l, hh), (w2h, hl))):
                            ins = pe.matmul(Y_BANK[2 * k + half], w[k2][0:rows, wc], v[t % 2 if isinstance(t, int) else k2][0:rows, cols],
                                            start=(first and n == 0), stop=(last and n == 2), skip_group_check=True)
                return ins

            for b in range(B - 1):
                second_rows_transposed(b)
            for b in range(B - 1):
                router_scores(b)
            keep_warm(5, O_BANK)
            second_rows_transposed(B - 1)
            hidden(0, 0, P, halves=(0,))
            router_scores(B - 1)
            pe.wait_ge(lgT_ok, 1)
            for t in range(TB):
                ins = pe.transpose(C_RT[:, t * P:(t + 1) * P], lgT[:, t * P:(t + 1) * P], ident[:, :])
            ins.then_inc(rt_mm, 1)
            hidden(0, 0, P, halves=(1,))
            pe.wait_ge(lg_ok, TB)
            for t in range(SHT - 1):
                hidden(t + 1, t + 1, P if t + 1 < SFULL else SREST)
                result(t, t, P, first=(t == 0)).then_inc(y_mm, 1)

            def gates_transposed(half):
                for c in range(NT // 2):
                    ins = pe.transpose(G_BANK[half][0:NE + NS, c * P:(c + 1) * P], gates[:, half * (NT // 2) + c, :], ident[:, :])
                ins.then_inc(gT_mm, 1)

            pe.wait_ge(gparts_ok, 1)
            for t in range(NT):
                ins = pe.transpose(G_BANK[0].bitcast(BF16)[0:3 * NE, t * P:(t + 1) * P],
                                   gparts[:, t].rearrange("p a e -> p (a e)"), ident_b[:, :])
            ins.then_inc(gT_mm, 1)
            gates_transposed(1)
            result(SHT - 1, SHT - 1, SREST).then_inc(y_mm, 1)
            pe.wait_ge(gT3_ok, 1)
            gates_transposed(0)
            pe.wait_ge(owner_ok, 1)
            hidden(SHT, SHT % 2, P, r=0)
            pe.wait_ge(b2_ld, 32)
            for k in range(KD):
                for half in range(2):
                    pe.matmul(Y_BANK[2 * k + half], b2_sb[:, k * P:(k + 1) * P],
                              gTf[:, half * HALF:(half + 1) * HALF], start=False, stop=False, skip_group_check=True)
            with pe.Fori(0, RT // 2 - 1) as it:
                for j in range(2):
                    t = it * 2 + (SHT + j)
                    hidden(t + 1, (SHT + j + 1) % 2, P, r=it * 2 + (j + 1))
                    result(t, (SHT + j) % 2, P).then_inc(y_mm, 1)
            hidden(TILES - 1, (TILES - 1) % 2, P, r=RT - 1)
            for half in range(2):
                result(TILES - 2, (TILES - 2) % 2, P, halves=(half,))
                result(TILES - 1, (TILES - 1) % 2, P, halves=(half,), last=True).then_inc(y_done, 1)
            for b in range(B):
                pe.wait_ge(yT_ok[b // (B // 2)], 2)
                for t in range(TB):
                    for k in range(KD):
                        n = (TB * b + t) * P
                        ins = pe.transpose(E_BANK[b][:, (t * KD + k) * P:(t * KD + k + 1) * P],
                                           yT[:, k, n:n + P], ident[:, :])
                ins.then_inc(yb_mm, 1)


_INS = ['x', 'ctx_1024', 'fside_BxSx2_0', 'g_xattn', 'g_ffn', 'L0_xattn_Wq', 'L0_xattn_Wkv', 'L0_xattn_Wout',
        'L0_xattn_bout', 'L0_ffn_sw1', 'L0_ffn_sb1', 'L0_ffn_sw2', 'L0_ffn_sb2', 'L0_ffn_rw1', 'L0_ffn_rb1',
        'L0_ffn_rw2', 'L0_ffn_rb2', 'L0_ffn_router_w', 'L0_ffn_router_b']
_OUTS = [((4, 256, 256), 'float32')]


def kernel(**inputs):
    import numpy as _np
    import concourse.bacc as _bacc
    from concourse import mybir as _mybir
    from concourse.bass_utils import run_bass_kernel_spmd as _run

    nc = _bacc.Bacc("TRN2", target_bir_lowering=False, num_devices=1)
    arrays, args = {}, []
    for name in _INS:
        a = _np.ascontiguousarray(inputs[name])
        arrays[f"in_{name}_dram"] = a
        args.append(nc.dram_tensor(f"in_{name}_dram", a.shape, _mybir.dt.from_np(a.dtype), kind="ExternalInput").ap())
    for i, (shape, dtype) in enumerate(_OUTS):
        dt = _mybir.dt.from_np(_np.dtype(dtype))
        args.append(nc.dram_tensor(f"out_{i}_dram", shape, dt, kind="ExternalOutput").ap())
    gated_cross_attention_moe(nc, *args)
    r = _run(nc, [arrays], core_ids=[0])
    got = tuple(r.results[0][f"out_{i}_dram"] for i in range(len(_OUTS)))
    return got[0]
```
